# Optimizing a Trainium2 kernel written in Bass

```python
import numpy as np
import jax
import jax.numpy as jnp

def _softmax(x, axis=-1):
    return jax.nn.softmax(x, axis=axis)

def _gelu(x):
    return jax.nn.gelu(x, approximate=True)

def _silu(x):
    return jax.nn.silu(x)

def _sigmoid(x):
    return jax.nn.sigmoid(x)

def _layernorm(x, axis=-1, eps=1e-05):
    m = jnp.mean(x, axis=axis, keepdims=True)
    v = jnp.var(x, axis=axis, keepdims=True)
    return (x - m) / jnp.sqrt(v + eps)

def _scatter_add(tgt, idx, src, axis=0):
    return tgt.at[idx].add(src)

def _segment_sum(src, seg, n):
    return jax.ops.segment_sum(src, seg, n)
kernel_name = 'mk_recurrent_d1_jaxref_r8_8d5eb6'

def setup_inputs(seed: int=0):
    np.random.seed(seed)
    _w = jnp.asarray

    def _L0_attn_setup():
        import jax, jax.numpy as jnp
        import numpy as np
        H = 512
        D_IN = 1024
        N = 16
        K = 4
        R = 32
        EPS = 1e-06

        def rms_forward(x, eps=EPS):
            xf = x.astype(jnp.float32)
            var = jnp.mean(xf * xf, axis=-1, keepdims=True)
            return (xf * jax.lax.rsqrt(var + eps)).astype(x.dtype)
        key = jax.random.key(seed)
        ks = jax.random.split(key, 10)
        s = 0.02
        hidden_states = jax.random.normal(ks[0], (2, 128, H), dtype=jnp.float32)
        W_in = jax.random.normal(ks[1], (2 * D_IN, H), dtype=jnp.float32) * s
        conv_w = jax.random.normal(ks[2], (D_IN, K), dtype=jnp.float32) * 0.2
        conv_b = jax.random.normal(ks[3], (D_IN,), dtype=jnp.float32) * 0.02
        W_x = jax.random.normal(ks[4], (R + 2 * N, D_IN), dtype=jnp.float32) * s
        W_dt = jax.random.normal(ks[5], (D_IN, R), dtype=jnp.float32) * s
        b_dt = jax.random.normal(ks[6], (D_IN,), dtype=jnp.float32) * 0.02
        A_log = jnp.log(jnp.broadcast_to(jnp.arange(1, N + 1, dtype=jnp.float32)[None, :], (D_IN, N)))
        D = jnp.ones((D_IN,), dtype=jnp.float32)
        W_out = jax.random.normal(ks[7], (H, D_IN), dtype=jnp.float32) * s
        return {'hidden_states': hidden_states, 'W_in': W_in, 'conv_w': conv_w, 'conv_b': conv_b, 'W_x': W_x, 'W_dt': W_dt, 'b_dt': b_dt, 'A_log': A_log, 'D': D, 'W_out': W_out}
    _L0_attn_in = _L0_attn_setup()

    def _L0_ffn_setup():
        import jax, jax.numpy as jnp
        import numpy as np
        TOP_K = 2
        key = jax.random.key(seed)
        k1, k2, k3 = jax.random.split(key, 3)
        B, S, H, O, E = (32, 1, 512, 512, 8)
        x = jax.random.normal(k1, (B, S, H), dtype=jnp.float32)
        gate_w = jax.random.normal(k2, (H, E), dtype=jnp.float32) * 0.02
        expert_w = jax.random.normal(k3, (E, H, O), dtype=jnp.float32) * 0.02
        return {'x': x, 'gate_w': gate_w, 'expert_w': expert_w}
    _L0_ffn_in = _L0_ffn_setup()
    _d = {'L0_attn_hidden_states': _L0_attn_in['hidden_states'], 'L0_attn_W_in': _L0_attn_in['W_in'], 'L0_attn_conv_w': _L0_attn_in['conv_w'], 'L0_attn_conv_b': _L0_attn_in['conv_b'], 'L0_attn_W_x': _L0_attn_in['W_x'], 'L0_attn_W_dt': _L0_attn_in['W_dt'], 'L0_attn_b_dt': _L0_attn_in['b_dt'], 'L0_attn_A_log': _L0_attn_in['A_log'], 'L0_attn_D': _L0_attn_in['D'], 'L0_attn_W_out': _L0_attn_in['W_out'], 'L0_ffn_gate_w': _L0_ffn_in['gate_w'], 'L0_ffn_expert_w': _L0_ffn_in['expert_w']}
    _x0 = _d['L0_attn_hidden_states']
    _d['L0_attn_hidden_states'] = jax.random.normal(jax.random.fold_in(jax.random.key(seed), 1), (2, 1024, 512), dtype=_x0.dtype)
    del _x0
    return _d

def reference(L0_attn_hidden_states, L0_attn_W_in, L0_attn_conv_w, L0_attn_conv_b, L0_attn_W_x, L0_attn_W_dt, L0_attn_b_dt, L0_attn_A_log, L0_attn_D, L0_attn_W_out, L0_ffn_gate_w, L0_ffn_expert_w):

    def _L0_attn_ref(hidden_states, W_in, conv_w, conv_b, W_x, W_dt, b_dt, A_log, D, W_out):
        import jax, jax.numpy as jnp
        import numpy as np
        H = 512
        D_IN = 1024
        N = 16
        K = 4
        R = 32
        EPS = 1e-06

        def rms_forward(x, eps=EPS):
            xf = x.astype(jnp.float32)
            var = jnp.mean(xf * xf, axis=-1, keepdims=True)
            return (xf * jax.lax.rsqrt(var + eps)).astype(x.dtype)
        b, L, _ = hidden_states.shape
        proj = hidden_states @ W_in.T
        x, gate = (proj[..., :D_IN], proj[..., D_IN:])
        xpad = jnp.pad(x, ((0, 0), (K - 1, 0), (0, 0)))
        xc = conv_b
        for j in range(K):
            xc = xc + conv_w[:, j] * xpad[:, j:j + L, :]
        x = jax.nn.silu(xc)
        ssm = x @ W_x.T
        ts, Bm, Cm = (ssm[..., :R], ssm[..., R:R + N], ssm[..., R + N:])
        ts = rms_forward(ts)
        Bm = rms_forward(Bm)
        Cm = rms_forward(Cm)
        dt = jax.nn.softplus(ts @ W_dt.T + b_dt)
        A = -jnp.exp(A_log.astype(jnp.float32))

        def step(state, inp):
            dt_t, B_t, C_t, u_t = inp
            dA = jnp.exp(dt_t[..., None] * A)
            state = state * dA + (dt_t * u_t)[..., None] * B_t[:, None, :]
            y = jnp.einsum('bdn,bn->bd', state, C_t)
            return (state, y)
        init = jnp.zeros((b, D_IN, N), dtype=jnp.float32)
        xs = (dt.transpose(1, 0, 2), Bm.transpose(1, 0, 2), Cm.transpose(1, 0, 2), x.transpose(1, 0, 2))
        _, ys = jax.lax.scan(step, init, xs)
        y = ys.transpose(1, 0, 2) + x * D
        y = y * jax.nn.silu(gate)
        return y @ W_out.T

    def _L0_ffn_ref(x, gate_w, expert_w):
        import jax, jax.numpy as jnp
        import numpy as np
        TOP_K = 2
        E = expert_w.shape[0]
        gate_logits = jnp.einsum('bsh,he->bse', x, gate_w)
        top_vals, top_idx = jax.lax.top_k(gate_logits, TOP_K)
        probs = jax.nn.softmax(top_vals, axis=-1)
        onehot = jax.nn.one_hot(top_idx, E, dtype=x.dtype)
        w_e = jnp.einsum('bsk,bske->bse', probs, onehot)
        expert_out = jnp.einsum('bsh,eho->bseo', x, expert_w)
        out = jnp.einsum('bseo,bse->bso', expert_out, w_e)
        return out
    x = L0_attn_hidden_states
    xn = _layernorm(x, axis=-1)
    s = _L0_attn_ref(xn, L0_attn_W_in, L0_attn_conv_w, L0_attn_conv_b, L0_attn_W_x, L0_attn_W_dt, L0_attn_b_dt, L0_attn_A_log, L0_attn_D, L0_attn_W_out)
    g = _silu(_L0_ffn_ref(xn, L0_ffn_gate_w, L0_ffn_expert_w))
    x = x + s * g
    return x

_drawn_inputs = setup_inputs


def setup_inputs(seed=0):
    import zlib

    import numpy as np

    out = dict(_drawn_inputs(seed))
    spreads = {'L0_attn_D': (1.0, 0.6)}
    factors = {'L0_attn_W_in': 5.904,
     'L0_attn_conv_w': 5.01,
     'L0_attn_conv_b': 8.0,
     'L0_attn_W_x': 5.56,
     'L0_attn_W_dt': 8.0,
     'L0_attn_b_dt': 8.0,
     'L0_attn_A_log': 8.0,
     'L0_attn_W_out': 5.007,
     'L0_ffn_gate_w': 5.901,
     'L0_ffn_expert_w': 5.058}
    for name, (base, spread) in spreads.items():
        noise = np.random.default_rng([zlib.crc32(name.encode()), seed]).standard_normal(out[name].shape)
        drawn = base * np.exp(spread * noise) if base else spread * noise
        out[name] = jnp.asarray(drawn.astype(out[name].dtype))
    for name, factor in factors.items():
        out[name] = (out[name] * factor).astype(out[name].dtype)
    return out
```

```python
from contextlib import ExitStack

import concourse.bass as bass
from concourse import mybir

F32 = mybir.dt.float32
ALU = mybir.AluOpType
ACT = mybir.ActivationFunctionType
AX_X = mybir.AxisListType.X

P = 128
BATCH, SEQ, H = 2, 1024, 512
D_IN, N, K, R, E = 1024, 16, 4, 32, 8
TOK = BATCH * SEQ
TC = 512
NCH = TOK // TC
PER_ROW = SEQ // TC
NT = D_IN // P
HK = H // P
TT = TC // P
NG = 4
NQ = N // NG
CH = P // NG
NR = P // CH
UNITS = NR * NQ
SSM = R + 2 * N
ONES_ROW = 64
RMS_EPS, LN_EPS = 1e-6, 1e-5
LNEXP, SILU = "natural_log_exp_and_others", "silu_and_others"
RING = 2
REP = 16 * NG
PAIRS = NT // 2
START = 1


def scan_moe(nc, x, win, wdt0, wx, wring, gate_w, a_log, conv_w, conv_b, d_skip, bc_dram, out):
    with ExitStack() as ctx:
        def sb(name, *shape):
            return ctx.enter_context(nc.sbuf_tensor(name, [P, *shape], F32))

        def ps(name, *shape):
            return ctx.enter_context(nc.psum_tensor(name, [P, *shape], F32))

        def sem(name):
            return ctx.enter_context(nc.semaphore(name))

        xnT = sb("xnT", HK, TOK)
        ring = sb("ring", 2 * RING * NQ, TC)
        decay, drive = ring[:, 0:RING * NQ, :], ring[:, RING * NQ:, :]
        w_ring = sb("w_ring", 2, HK, H)
        w_rec = sb("w_rec", 2 * HK + 1, P)
        w_dt0 = sb("w_dt0", P)
        w_x = sb("w_x", NT, SSM)
        w_gate = sb("w_gate", HK, E)
        xy = sb("xy", 2, NT, TC)
        gate = sb("gate", 2, TC)
        moe = sb("moe", TT, H)
        rep = sb("rep", 2, NR, 2, TC)
        b_all, c_all = sb("b_all", NQ, TC), sb("c_all", NQ, TC)
        x_pad = sb("x_pad", TC + K - 1)
        z = sb("z", 2, TC)
        halo = sb("halo", NT, K - 1)
        t_e, t_l = sb("t_e", TC), sb("t_l", TC)
        dtu = sb("dtu", 2, TC)
        dt, u = dtu[:, 0, :], dtu[:, 1, :]
        dt_in = sb("dt_in", TC)
        part = sb("part", 2, H)
        y_t = sb("y_t", TC)
        res = sb("res", H)
        state = sb("state", NT * UNITS)
        a_neg = sb("a_neg", NT * UNITS)
        cw, cb, dsk = sb("cw", NT * K), sb("cb", NT), sb("dsk", NT)
        ident = sb("ident", P)
        stack = sb("stack", CH)
        w_e = sb("w_e", 16, E)
        spare = [rep[:, 1, r, 0, :] for r in range(NR)]
        ident_i, stats, mv = spare[0][:, 0:P], spare[1][:, 0:96], spare[1][:, 96:128]
        stats, mv = stats.rearrange("p (k f) -> p k f", f=6), mv.rearrange("p (k f) -> p k f", f=2)
        nv, nl, nr, nt_, m1 = (spare[1][:, 128 + 16 * k:144 + 16 * k] for k in range(5))
        logit, rank, cmp_ = (spare[2][:, 128 * k:128 * (k + 1)].rearrange("p (t e) -> p t e", e=E) for k in range(3))
        ssm = sb("ssm", TT, SSM)
        sq = y_t[:, 0:TT * SSM].rearrange("p (t f) -> p t f", f=SSM)
        grp = sb("grp", TT, SSM // N)
        rv, rl, rr, rt = sb("rv", TT, 3), sb("rl", TT, 3), sb("rr", TT, 3), sb("rt", TT, 3)

        y_ps, f_ps = ps("y_ps", 2, TC), ps("f_ps", 2, TC)
        x_ps, g_ps, dt_ps, o_ps = ps("x_ps", TC), ps("g_ps", TC), ps("dt_ps", TC), ps("o_ps", TC)

        s_const = sem("s_const")
        s_x = [sem(f"s_x{g}") for g in range(NCH)]
        s_rec = sem("s_rec")
        s_wr = [sem(f"s_wr{s}") for s in range(2)]
        s_bc0 = sem("s_bc0")
        s_bc = sem("s_bc")
        s_rep = [[sem(f"s_rep{s}{r}") for r in range(NR)] for s in range(2)]
        s_res = sem("s_res")
        s_out = sem("s_out")
        id_zero, id_ok = sem("id_zero"), sem("id_ok")
        stack_ok = sem("stack_ok")
        a_exp, a_ok = sem("a_exp"), sem("a_ok")
        dve_link, act_link = sem("dve_link"), sem("act_link")
        ln_v, ln_r = sem("ln_v"), sem("ln_r")
        xn_ok = sem("xn_ok")
        tr_mm, tr_ev = sem("tr_mm"), sem("tr_ev")
        lg_mm = sem("lg_mm")
        lg_d, lg_e, we_ok = sem("lg_d"), sem("lg_e"), sem("we_ok")
        x_mm, x_ev = sem("x_mm"), sem("x_ev")
        conv_ok = sem("conv_ok")
        x_ok = sem("x_ok")
        g_mm, g_ev, g_ok = sem("g_mm"), sem("g_ev"), sem("g_ok")
        ssm_mm, ssm_v, ssm_r = sem("ssm_mm"), sem("ssm_v"), sem("ssm_r")
        ssm_ok, ssmT_mm, dtin_ok = sem("ssm_ok"), sem("ssmT_mm"), sem("dtin_ok")
        dt_mm, dt_ln, dt_ok = sem("dt_mm"), sem("dt_ln"), sem("dt_ok")
        decay_ok = sem("decay_ok")
        drive_ok = sem("drive_ok")
        scan_ok = sem("scan_ok")
        prod_ok = sem("prod_ok")
        sum_ok = sem("sum_ok")
        gated = sem("gated")
        f_mm = sem("f_mm")
        f_ev = sem("f_ev")
        f_add = sem("f_add")
        moe_ok = sem("moe_ok")
        moe_clear = sem("moe_clear")
        o_mm, o_mul, o_add = sem("o_mm"), sem("o_mul"), sem("o_add")
        chunk_ready = sem("chunk_ready")

        x_t = x.rearrange("(n p) h -> n p h", p=P)
        out_t = out.rearrange("(n p) h -> n p h", p=P)
        b_rows = R + N
        block = ctx.enter_context(nc.Block())

        def in_pairs(eng, chunk_body):
            with eng.Fori(0, PAIRS - 1) as pr:
                chunk_body(pr, False)
            chunk_body(PAIRS - 1, True)

        @block.sync
        def _(sp):
            for dst, src in ((a_neg[:, :], a_log), (w_x[:, :, :], wx), (w_gate[:, :, :], gate_w),
                             (cw[:, :], conv_w), (cb[:, :], conv_b), (dsk[:, :], d_skip), (w_dt0[:, :], wdt0)):
                sp.dma_start(dst, src).then_inc(s_const, 16)
            for g in range(NCH):
                for i in range(TT):
                    sp.dma_start(ring[:, g * TT + i, :], x_t[g * TT + i]).then_inc(s_x[g], 16)
            sp.dma_start(w_rec[:, :, :], win[0]).then_inc(s_rec, 16)
            sp.dma_start(w_ring[:, 0, :, :], wring[0]).then_inc(s_wr[0], 16)

            for t in range(NT):
                sp.wait_ge(x_mm, t + 1)
                sp.wait_ge(s_rec, 16 * t + 16)
                sp.dma_start(w_rec[:, :, :], win[t + 1]).then_inc(s_rec, 16)

            def value(v):
                return v if isinstance(v, int) else sp.snap(v)

            def spread(s, stepped, used):
                sp.wait_ge(dt_ok, stepped)
                if used is not None:
                    sp.wait_ge(decay_ok, used)
                    sp.wait_ge(drive_ok, used)
                for r in range(NR):
                    for g in range(NG):
                        sp.dma_start(rep[CH * g:CH * (g + 1), s, r, :, :],
                                     dtu[CH * r:CH * (r + 1), :, :]).then_inc(s_rep[s][r], 16)

            def store(c, i):
                k = TT * c + i
                sp.wait_ge(o_add, k + 1)
                sp.dma_start(out_t[k], moe[:, i, :]).then_inc(s_out, 16)

            def load_residual(c, i):
                k = TT * c + i
                sp.wait_ge(o_add, k)
                sp.dma_start(res[:, :], x_t[k]).then_inc(s_res, 16)

            def finish(c):
                for i in range(TT):
                    load_residual(c, i)
                    if i >= 1:
                        store(c, i - 1)
                store(c, TT - 1)
                if c < NCH - 1:
                    sp.wait_ge(o_mm, TT * (c + 1))
                    sp.dma_start(w_ring[:, 0, :, :], wring[0]).then_inc(s_wr[0], 16)

            for c in range(NCH):
                sp.wait_ge(dtin_ok, c + 1)
                sp.dma_start(bc_dram[c], dt_in[R:R + 2 * N, :]).then_inc(s_bc0, 16)
                sp.wait_ge(s_bc0, 16 * (c + 1))
                if c:
                    sp.wait_ge(prod_ok, RING + NR * NT * c)
                for k, dst in ((0, b_all), (N, c_all)):
                    for g in range(NG):
                        rows = bc_dram[c, k + NQ * g:k + NQ * (g + 1), :].rearrange("(o q) t -> o q t", o=1)
                        sp.dma_start(dst[CH * g:CH * (g + 1), :, :],
                                     rows.broadcast_to([CH, NQ, TC])).then_inc(s_bc, 16)
                spread(0, NT * c + 1, UNITS * (NT * c - 1) if c else None)
                if c:
                    finish(c - 1)

                def body(pr, last, c=c):
                    for s in range(2):
                        t = pr * 2 + s
                        n = NT * c + t
                        tiles, landed = value(n + 1), value(16 * (NT + n + 1))
                        x_tiles, experts = value(NT * (c + 1) + t + 1), value(TT * n)
                        stepped, used = value(n + 2), value(UNITS * n)
                        record, expert = value(t + 1), value(t + 1)
                        sp.wait_ge(g_mm, tiles)
                        if c < NCH - 1:
                            sp.wait_ge(x_mm, x_tiles)
                        sp.wait_ge(f_mm, experts)
                        sp.wait_ge(s_rec, landed)
                        if not (last and s == 1):
                            spread(1 - s, stepped, used)
                        sp.dma_start(w_rec[:, :, :], win[record]).then_inc(s_rec, 16)
                        sp.dma_start(w_ring[:, 1 - s, :, :], wring[expert]).then_inc(s_wr[1 - s], 16)
                for pr in range(PAIRS):
                    body(pr, pr == PAIRS - 1)
                sp.wait_ge(f_mm, TT * NT * (c + 1))
                sp.dma_start(w_ring[:, 1, :, :], wring[E + 1]).then_inc(s_wr[1], 16)
            finish(NCH - 1)
            sp.wait_ge(s_out, 16 * (TOK // P))

        @block.gpsimd
        def _(pool):
            pool.memset(ident_i[:, :], 0.0).then_inc(id_zero, 1)
            pool.wait_ge(id_zero, 1)
            pool.affine_select(out=ident[:, :], in_=ident_i[:, :], compare_op=ALU.not_equal, fill=1.0, base=0,
                               pattern=[[-1, P]], channel_multiplier=1).then_inc(id_ok, 1)
            pool.memset(moe[:, :, :], 0.0).then_inc(moe_clear, 1)
            pool.sem_inc(f_add, 2)

            for c in range(NCH):
                pool.wait_ge(s_bc, 16 * 2 * NG * (c + 1))
                pool.wait_ge(moe_clear, c + 1)

                def body(pr, last, c=c):
                    for s in range(2):
                        t = pr * 2 + s
                        n = NT * c + t
                        for r in range(NR):
                            pool.wait_ge(prod_ok, NR * n + r + 1)
                            pool.wait_ge(s_rep[s][r], REP * (PAIRS * c + pr + 1))
                            for q in range(NQ):
                                pool.tensor_tensor(drive[:, NQ * (r % RING) + q, :], rep[:, s, r, 1, :],
                                                   b_all[:, q, :], ALU.mult).then_inc(drive_ok, 1)
                            k = TT * (NT * c + t) + r
                            pool.wait_ge(f_ev, k + 3)
                            if c:
                                pool.wait_ge(f_add, k + 3 - TT)
                            else:
                                pool.wait_ge(f_add, k + 2)
                            pool.tensor_tensor(moe[:, r, :], moe[:, r, :], part[:, r % 2, :],
                                               ALU.add).then_inc(f_add, 1)
                in_pairs(pool, body)

                for i in range(TT):
                    k = TT * c + i
                    pool.wait_ge(o_mul, k + 1)
                    pool.wait_ge(s_res, 16 * (k + 1))
                    pool.tensor_tensor(moe[:, i, :], moe[:, i, :], res[:, :], ALU.add).then_inc(o_add, 1)
                if c < NCH - 1:
                    pool.wait_ge(s_out, 16 * TT * (c + 1))
                    pool.memset(moe[:, :, :], 0.0).then_inc(moe_clear, 1)

        @block.scalar
        def _(act):
            links = [0]

            act.sem_inc(f_ev, 2)
            for s in (x_ev, x_ok, g_ev):
                act.sem_inc(s, START)
            act.preload_act_table_set(LNEXP)
            act.wait_ge(s_const, 16 * 7)
            act.activation(a_neg[:, :], a_neg[:, :], ACT.Exp).then_inc(a_exp, 1)

            def rsqrt_guess(src, tmp, dst, done, link_at):
                act.activation(tmp, src, ACT.Ln).then_inc(act_link, 1)
                act.wait_ge(act_link, link_at)
                act.activation(dst, tmp, ACT.Exp, scale=-0.5).then_inc(done, 1)

            act.wait_ge(ln_v, 1)
            links[0] += 1
            rsqrt_guess(nv, nl, nr, ln_r, links[0])
            for k in range(16):
                act.wait_ge(tr_mm, k + 1)
                act.copy(xnT[:, :, P * k:P * (k + 1)],
                         f_ps[:, k % 2, :].rearrange("p (k t) -> p k t", k=HK)).then_inc(tr_ev, 1)
            act.wait_ge(lg_d, 1)
            act.activation(w_e[:, :, :], logit[:, :, :], ACT.Exp).then_inc(lg_e, 1)

            def copy_x(c, t):
                j = NT * c + t
                act.wait_ge(x_mm, j + 1)
                act.wait_ge(conv_ok, START + j)
                act.copy(x_pad[:, K - 1:], x_ps[:, :]).then_inc(x_ev, 1)

            def silu_x(c, t, s):
                j = NT * c + t
                act.wait_ge(conv_ok, START + j + 1)
                act.activation(xy[:, c % 2, t, :], z[:, s, :], ACT.Silu).then_inc(x_ok, 1)

            act.preload_act_table_set(SILU)
            with act.Fori(0, PAIRS) as pr:
                for s in range(2):
                    copy_x(0, pr * 2 + s)
                    silu_x(0, pr * 2 + s, s)
            act.preload_act_table_set(LNEXP)

            def step_sizes(n, links_at):
                act.wait_ge(dt_mm, n + 1)
                act.wait_ge(dt_ok, n)
                act.activation(t_e[:, :], dt_ps[:, :], ACT.Abs).then_inc(act_link, 1)
                act.wait_ge(act_link, links_at + 1)
                act.activation(t_e[:, :], t_e[:, :], ACT.Exp, scale=-1.0).then_inc(act_link, 1)
                act.wait_ge(act_link, links_at + 2)
                act.activation(t_l[:, :], t_e[:, :], ACT.Ln, bias=1.0).then_inc(dt_ln, 1)

            def decays(c, t, pr, s, r):
                n = NT * c + t
                act.wait_ge(s_rep[s][r], REP * (PAIRS * c + pr + 1))
                act.wait_ge(sum_ok, NR * n + r + 1)
                for q in range(NQ):
                    act.activation(decay[:, NQ * (r % RING) + q, :], rep[:, s, r, 0, :], ACT.Exp,
                                   scale=a_neg[:, bass.ds(t * UNITS + r * NQ + q, 1)]).then_inc(decay_ok, 1)

            def weigh_expert(c, t, i):
                k = TT * (NT * c + t) + i
                act.wait_ge(f_mm, k + 1)
                act.wait_ge(f_add, k + 1)
                act.activation(part[:, i % 2, :], f_ps[:, i % 2, :], ACT.Copy,
                               scale=w_e[:, TT * c + i, bass.ds(t, 1)]).then_inc(f_ev, 1)

            act.wait_ge(a_ok, 1)
            act.wait_ge(we_ok, 1)
            for c in range(NCH):
                act.wait_ge(ssm_v, c + 1)
                links[0] += 1
                rsqrt_guess(rv[:, :, :], rl[:, :, :], rr[:, :, :], ssm_r, links[0])
                if c:
                    act.wait_ge(f_add, 2 + TT * NT * c)
                    act.preload_act_table_set(SILU)
                    act.activation(moe[:, :, :], moe[:, :, :], ACT.Silu).then_inc(moe_ok, 1)
                    act.preload_act_table_set(LNEXP)
                step_sizes(NT * c, links[0])
                links[0] += 2
                start = links[0]

                def body(pr, last, c=c, start=start):
                    for s in range(2):
                        t = pr * 2 + s
                        n = NT * c + t
                        decays(c, t, pr, s, 0)
                        act.wait_ge(g_mm, n + 1)
                        if s == 0:
                            act.wait_ge(gated, START + n)
                        act.copy(gate[:, s, :], g_ps[:, :]).then_inc(g_ev, 1)
                        if c < NCH - 1:
                            copy_x(c + 1, t)
                        decays(c, t, pr, s, 1)
                        if not (last and s == 1):
                            step_sizes(n + 1, start + 2 * t)
                        weigh_expert(c, t, 0)
                        decays(c, t, pr, s, 2)
                        weigh_expert(c, t, 1)
                        if s == 1:
                            act.preload_act_table_set(SILU)
                            if c < NCH - 1:
                                if c >= 1:
                                    act.wait_ge(o_mm, TT * c)
                                for v in range(2):
                                    silu_x(c + 1, pr * 2 + v, v)
                            act.wait_ge(g_ev, START + n + 1)
                            for v in range(2):
                                act.activation(gate[:, v, :], gate[:, v, :], ACT.Silu).then_inc(g_ok, 1)
                            act.preload_act_table_set(LNEXP)
                        decays(c, t, pr, s, 3)
                        weigh_expert(c, t, 2)
                        weigh_expert(c, t, 3)
                in_pairs(act, body)
                links[0] += 2 * (NT - 1)
            act.wait_ge(f_add, 2 + TT * NT * NCH)
            act.preload_act_table_set(SILU)
            act.activation(moe[:, :, :], moe[:, :, :], ACT.Silu).then_inc(moe_ok, 1)

        @block.vector
        def _(dve):
            links = [0]

            def link(ins):
                links[0] += 1
                ins.then_inc(dve_link, 1)
                dve.wait_ge(dve_link, links[0])

            def newton(v, r, t):
                link(dve.tensor_tensor(t, v, r, ALU.mult))
                link(dve.tensor_tensor(t, t, r, ALU.mult))
                link(dve.tensor_scalar(t, t, -0.5, 1.5, ALU.mult, ALU.add))
                link(dve.tensor_tensor(r, r, t, ALU.mult))

            dve.sem_inc(prod_ok, RING)
            for s in (conv_ok, gated):
                dve.sem_inc(s, START)
            dve.memset(dt_in[:, :], 1.0).then_inc(dve_link, 1)
            dve.memset(halo[:, :, :], 0.0).then_inc(dve_link, 1)
            links[0] += 2
            for g in range(NCH):
                dve.wait_ge(s_x[g], 16 * TT)
                for i in range(TT):
                    link_last = dve.bn_stats(stats[:, g * TT + i, :], ring[:, g * TT + i, :])
                    link_last.then_inc(dve_link, 1)
                    links[0] += 1
            dve.wait_ge(dve_link, links[0])
            for k in range(16):
                dve.bn_aggr(mv[:, k, :], stats[:, k, :]).then_inc(dve_link, 1)
                links[0] += 1
            dve.wait_ge(dve_link, links[0])
            link(dve.tensor_scalar(nv, mv[:, :, 1], LN_EPS, None, ALU.add))
            dve.sem_inc(ln_v, 1)
            dve.wait_ge(ln_r, 1)
            newton(nv, nr, nt_)
            for k in range(16):
                dve.tensor_scalar(ring[:, k, :], ring[:, k, :], mv[:, k, 0:1], nr[:, k:k + 1],
                                  ALU.subtract, ALU.mult).then_inc(xn_ok, 1)
            dve.wait_ge(id_ok, 1)
            link(dve.tensor_reduce(stack[:, :], ident[:, :].rearrange("p (g c) -> p c g", g=NG), AX_X, ALU.add))
            dve.sem_inc(stack_ok, 1)
            dve.wait_ge(a_exp, 1)
            dve.tensor_scalar(a_neg[:, :], a_neg[:, :], -1.0, None, ALU.mult).then_inc(a_ok, 1)

            dve.wait_ge(lg_mm, 1)
            link(dve.tensor_copy(logit[:, :, :], o_ps[:, 0:16 * E].rearrange("p (t e) -> p t e", e=E)))
            link(dve.tensor_reduce(m1, logit[:, :, :], AX_X, ALU.max))
            link(dve.memset(rank[:, :, :], 0.0))
            for e in range(E):
                if e:
                    dve.tensor_tensor(cmp_[:, :, 0:e], logit[:, :, e:e + 1].broadcast_to([P, 16, e]),
                                      logit[:, :, 0:e], ALU.is_gt).then_inc(dve_link, 1)
                    links[0] += 1
                dve.tensor_tensor(cmp_[:, :, e:E], logit[:, :, e:e + 1].broadcast_to([P, 16, E - e]),
                                  logit[:, :, e:E], ALU.is_ge).then_inc(dve_link, 1)
                links[0] += 1
                dve.wait_ge(dve_link, links[0])
                link(dve.tensor_tensor(rank[:, :, :], rank[:, :, :], cmp_[:, :, :], ALU.add))
            link(dve.tensor_tensor(logit[:, :, :], logit[:, :, :],
                                   m1.rearrange("p (t o) -> p t o", o=1).broadcast_to([P, 16, E]),
                                   ALU.subtract))
            dve.sem_inc(lg_d, 1)
            link(dve.tensor_scalar(rank[:, :, :], rank[:, :, :], 2.0, None, ALU.is_le))
            dve.wait_ge(lg_e, 1)
            link(dve.tensor_tensor(w_e[:, :, :], w_e[:, :, :], rank[:, :, :], ALU.mult))
            link(dve.tensor_reduce(m1, w_e[:, :, :], AX_X, ALU.add))
            link(dve.reciprocal(m1, m1))
            dve.tensor_tensor(w_e[:, :, :], w_e[:, :, :],
                              m1.rearrange("p (t o) -> p t o", o=1).broadcast_to([P, 16, E]),
                              ALU.mult).then_inc(we_ok, 1)

            def convolve(c, t, s, at):
                j = NT * c + t
                dve.wait_ge(x_ev, START + j + 1)
                dve.tensor_scalar(x_pad[:, 0:K - 1], halo[:, t, :], 1.0, None, ALU.mult).then_inc(dve_link, 1)
                dve.wait_ge(dve_link, at + 1)
                dve.tensor_scalar(halo[:, t, :], x_pad[:, TC:TC + K - 1], 1.0, None, ALU.mult).then_inc(dve_link, 1)
                if s == 0:
                    dve.wait_ge(x_ok, START + j)
                dve.tensor_scalar(z[:, s, :], x_pad[:, 0:TC], cw[:, bass.ds(t * K, 1)], cb[:, bass.ds(t, 1)],
                                  ALU.mult, ALU.add).then_inc(dve_link, 1)
                for k in range(1, K):
                    dve.wait_ge(dve_link, at + 2 + k)
                    last = dve.scalar_tensor_tensor(out=z[:, s, :], in0=x_pad[:, k:k + TC],
                                                    scalar=cw[:, bass.ds(t * K + k, 1)], in1=z[:, s, :],
                                                    op0=ALU.mult, op1=ALU.add)
                    last.then_inc(dve_link if k < K - 1 else conv_ok, 1)
            CONV_LINKS = K + 1

            dve.wait_ge(dve_link, links[0])
            with dve.Fori(0, PAIRS) as pr:
                for s in range(2):
                    convolve(0, pr * 2 + s, s, links[0] + CONV_LINKS * (pr * 2 + s))
            links[0] += CONV_LINKS * NT

            def step_sizes(c, t, spread, tiles, at):
                n = NT * c + t
                dve.wait_ge(dt_ln, n + 1)
                dve.wait_ge(gated, START + tiles)
                dve.tensor_scalar(y_t[:, :], t_e[:, :], 1.0, -1.0, ALU.add, ALU.add).then_inc(dve_link, 1)
                dve.wait_ge(dve_link, at + 1)
                dve.tensor_tensor(t_e[:, :], t_e[:, :], y_t[:, :], ALU.subtract).then_inc(dve_link, 1)
                dve.wait_ge(dve_link, at + 2)
                dve.tensor_tensor(t_l[:, :], t_l[:, :], t_e[:, :], ALU.add).then_inc(dve_link, 1)
                dve.wait_ge(dve_link, at + 3)
                if spread is not None:
                    for r in range(NR):
                        dve.wait_ge(s_rep[spread[0]][r], REP * spread[1])
                dve.scalar_tensor_tensor(out=dt[:, :], in0=dt_ps[:, :], scalar=0.0, in1=t_l[:, :],
                                         op0=ALU.max, op1=ALU.add).then_inc(dve_link, 1)
                dve.wait_ge(dve_link, at + 4)
                dve.wait_ge(x_ok, START + NT * (c + 1))
                dve.tensor_tensor(u[:, :], dt[:, :], xy[:, c % 2, t, :], ALU.mult).then_inc(dt_ok, 1)
            DT_LINKS = 4

            def quad(c, t, s, r):
                n = NT * c + t
                m = NR * n + r
                lo = NQ * (r % RING)
                for q in range(NQ):
                    dve.wait_ge(decay_ok, UNITS * n + NQ * r + q + 1)
                    dve.wait_ge(drive_ok, UNITS * n + NQ * r + q + 1)
                    dve.tensor_tensor_scan(drive[:, lo + q, :], decay[:, lo + q, :], drive[:, lo + q, :],
                                           state[:, bass.ds(t * UNITS + r * NQ + q, 1)],
                                           ALU.mult, ALU.add).then_inc(scan_ok, 1)
                dve.wait_ge(scan_ok, NQ * (m + 1))
                dve.tensor_scalar(state[:, bass.ds(t * UNITS + r * NQ, NQ)], drive[:, lo:lo + NQ, TC - 1], 1.0, None,
                                  ALU.mult).then_inc(dve_link, 1)
                dve.tensor_tensor(decay[:, lo:lo + NQ, :], drive[:, lo:lo + NQ, :], c_all[:, :, :],
                                  ALU.mult).then_inc(prod_ok, 1)

            def gate_tile(c, t, s, at):
                n = NT * c + t
                dve.wait_ge(sum_ok, RING + NR * (n + 1))
                dve.wait_ge(gated, START + n)
                dve.scalar_tensor_tensor(out=y_t[:, :], in0=xy[:, c % 2, t, :], scalar=dsk[:, bass.ds(t, 1)],
                                         in1=y_ps[:, s, :], op0=ALU.mult, op1=ALU.add).then_inc(dve_link, 1)
                dve.wait_ge(dve_link, at + 1)
                dve.wait_ge(g_ok, n + 1)
                dve.tensor_tensor(xy[:, c % 2, t, :], y_t[:, :], gate[:, s, :], ALU.mult).then_inc(gated, 1)

            def out_tile(c, i):
                k = TT * c + i
                dve.wait_ge(o_mm, k + 1)
                dve.wait_ge(moe_ok, c + 1)
                dve.tensor_tensor(moe[:, i, :], o_ps[:, :], moe[:, i, :], ALU.mult).then_inc(o_mul, 1)

            for c in range(NCH):
                dve.wait_ge(ssm_mm, c + 1)
                flat = "p t f -> p (t f)"
                link(dve.tensor_copy(ssm[:, :, :].rearrange(flat), x_ps[:, 0:TT * SSM]))
                link(dve.tensor_tensor(sq[:, :, :], ssm[:, :, :], ssm[:, :, :], ALU.mult))
                link(dve.tensor_reduce(grp[:, :, :].rearrange(flat),
                                       sq[:, :, :].rearrange("p t (g f) -> p (t g) f", f=N), AX_X, ALU.add))
                link(dve.tensor_tensor(rv[:, :, 0], grp[:, :, 0], grp[:, :, 1], ALU.add))
                link(dve.tensor_scalar(rv[:, :, 0], rv[:, :, 0], 1.0 / R, RMS_EPS, ALU.mult, ALU.add))
                link(dve.tensor_scalar(rv[:, :, 1:3], grp[:, :, 2:4], 1.0 / N, RMS_EPS, ALU.mult, ALU.add))
                dve.sem_inc(ssm_v, 1)
                dve.wait_ge(ssm_r, c + 1)
                newton(rv[:, :, :].rearrange(flat), rr[:, :, :].rearrange(flat), rt[:, :, :].rearrange(flat))
                link(dve.tensor_tensor(ssm[:, :, 0:R], ssm[:, :, 0:R],
                                       rr[:, :, 0:1].broadcast_to([P, TT, R]), ALU.mult))
                for k in range(2):
                    lo = R + N * k
                    link(dve.tensor_tensor(ssm[:, :, lo:lo + N], ssm[:, :, lo:lo + N],
                                           rr[:, :, k + 1:k + 2].broadcast_to([P, TT, N]), ALU.mult))
                dve.sem_inc(ssm_ok, 1)
                if c:
                    out_tile(c - 1, 0)
                dve.wait_ge(ssmT_mm, c + 1)
                if c:
                    dve.wait_ge(s_bc0, 16 * c)
                dve.tensor_copy(dt_in[0:SSM, :], dt_ps[0:SSM, :]).then_inc(dtin_ok, 1)
                if c:
                    out_tile(c - 1, 1)
                if c % PER_ROW == 0:
                    link(dve.memset(state[:, :], 0.0))
                if (c + 1) % PER_ROW == 0:
                    link(dve.memset(halo[:, :, :], 0.0))
                step_sizes(c, 0, (1, PAIRS * c) if c else None, NT * c, links[0])
                links[0] += DT_LINKS
                if c:
                    out_tile(c - 1, 2)
                    out_tile(c - 1, 3)
                dve.wait_ge(s_bc, 16 * 2 * NG * (c + 1))

                conv = CONV_LINKS if c < NCH - 1 else 0
                per_pair = 2 * (NR + DT_LINKS + conv + 1)
                start = links[0]

                def body(pr, last, c=c, conv=conv, start=start, per_pair=per_pair):
                    at = start + pr * per_pair
                    for s in range(2):
                        t = pr * 2 + s
                        quad(c, t, s, 0)
                        at = at + 1
                        if not (last and s == 1):
                            step_sizes(c, t + 1, (s, PAIRS * c + pr + 1),
                                       NT * c + pr * 2, at)
                            at = at + DT_LINKS
                        quad(c, t, s, 1)
                        at = at + 1
                        if conv:
                            convolve(c + 1, t, s, at)
                            at = at + conv
                        quad(c, t, s, 2)
                        quad(c, t, s, 3)
                        at = at + 2
                    for s in range(2):
                        gate_tile(c, pr * 2 + s, s, at)
                        at = at + 1
                in_pairs(dve, body)
                links[0] = start + per_pair * PAIRS - DT_LINKS
            for i in range(TT):
                out_tile(NCH - 1, i)

        @block.tensor
        def _(pe):
            pe.sem_inc(sum_ok, RING)
            pe.wait_ge(id_ok, 1)
            for k in range(16):
                pe.wait_ge(xn_ok, k + 1)
                if k >= 2:
                    pe.wait_ge(tr_ev, k - 1)
                for h in range(HK):
                    last = pe.transpose(f_ps[:, k % 2, P * h:P * (h + 1)], ring[:, k, P * h:P * (h + 1)], ident[:, :])
                last.then_inc(tr_mm, 1)
            pe.wait_ge(s_const, 16 * 7)
            pe.wait_ge(tr_ev, 16)
            for k in range(16):
                for h in range(HK):
                    last = pe.matmul(o_ps[:, E * k:E * (k + 1)], xnT[:, h, P * k:P * (k + 1)], w_gate[:, h, :],
                                     start=(h == 0), stop=(h == HK - 1))
            last.then_inc(lg_mm, 1)

            def project_x(c, t):
                j = NT * c + t
                pe.wait_ge(x_ev, START + j)
                for h in range(HK):
                    last = pe.matmul(x_ps[:, :], w_rec[:, h, :], xnT[:, h, TC * c:TC * (c + 1)],
                                     start=(h == 0), stop=(h == HK - 1))
                last.then_inc(x_mm, 1)

            with pe.Fori(0, NT) as t:
                pe.wait_ge(s_rec, 16 * (t + 1))
                project_x(0, t)

            def step_sizes(n, w):
                pe.wait_ge(dt_ok, n)
                pe.matmul(dt_ps[:, :], w, dt_in[:, :], start=True, stop=True).then_inc(dt_mm, 1)

            def out_tile(c, i):
                k = TT * c + i
                if k >= 1:
                    pe.wait_ge(o_mul, k)
                if i == 0:
                    pe.wait_ge(gated, START + NT * (c + 1))
                for t in range(NT):
                    if i == 0 and t % HK == 0:
                        pe.wait_ge(s_wr[t // HK], 16 * (5 * c + 5))
                    last = pe.matmul(o_ps[:, :], xy[:, c % 2, t, P * i:P * (i + 1)], w_ring[:, t // HK, t % HK, :],
                                     start=(t == 0), stop=(t == NT - 1))
                last.then_inc(o_mm, 1)

            def expert(c, t, pr, s, i):
                k = TT * (NT * c + t) + i
                if i == 0:
                    pe.wait_ge(s_wr[s], 16 * (5 * c + pr + 1))
                pe.wait_ge(f_ev, k + 1)
                for h in range(HK):
                    lo = TC * c + P * i
                    last = pe.matmul(f_ps[:, i % 2, :], xnT[:, h, lo:lo + P], w_ring[:, s, h, :],
                                     start=(h == 0), stop=(h == HK - 1))
                last.then_inc(f_mm, 1)

            def sum_states(c, t, s, r):
                m = NR * (NT * c + t) + r
                if r == 0:
                    pe.wait_ge(gated, START + NT * c + t - s)
                pe.wait_ge(prod_ok, RING + m + 1)
                for q in range(NQ):
                    last = pe.matmul(y_ps[CH * r:CH * (r + 1), s, :], stack[:, :], decay[:, NQ * (r % RING) + q, :],
                                     start=(q == 0), stop=(q == NQ - 1))
                last.then_inc(sum_ok, 1)

            pe.wait_ge(stack_ok, 1)
            for c in range(NCH):
                pe.wait_ge(x_ok, START + NT * (c + 1))
                pe.wait_ge(x_ev, START + NT * (c + 1))
                for i in range(TT):
                    for t in range(NT):
                        last = pe.matmul(x_ps[:, SSM * i:SSM * (i + 1)], xy[:, c % 2, t, P * i:P * (i + 1)],
                                         w_x[:, t, :], start=(t == 0), stop=(t == NT - 1))
                last.then_inc(ssm_mm, 1)
                if c:
                    out_tile(c - 1, 0)
                pe.wait_ge(ssm_ok, c + 1)
                pe.wait_ge(dt_ok, NT * c)
                for i in range(TT):
                    last = pe.transpose(dt_ps[0:SSM, P * i:P * (i + 1)], ssm[:, i, :], ident[:, :])
                last.then_inc(ssmT_mm, 1)
                if c:
                    out_tile(c - 1, 1)
                pe.wait_ge(dtin_ok, c + 1)
                step_sizes(NT * c, w_dt0[:, :])
                if c:
                    out_tile(c - 1, 2)
                    out_tile(c - 1, 3)

                def body(pr, last, c=c):
                    for s in range(2):
                        t = pr * 2 + s
                        n = NT * c + t
                        pe.wait_ge(s_rec, 16 * (NT + n + 1))
                        pe.wait_ge(g_ev, START + n)
                        for h in range(HK):
                            mm = pe.matmul(g_ps[:, :], w_rec[:, HK + h, :], xnT[:, h, TC * c:TC * (c + 1)],
                                           start=(h == 0), stop=(h == HK - 1))
                        mm.then_inc(g_mm, 1)
                        if not (last and s == 1):
                            step_sizes(n + 1, w_rec[:, 2 * HK, :])
                        if c < NCH - 1:
                            project_x(c + 1, t)
                        for r in range(NR):
                            expert(c, t, pr, s, r)
                            sum_states(c, t, s, r)
                in_pairs(pe, body)
            for i in range(TT):
                out_tile(NCH - 1, i)


def kernel(**inputs):
    import numpy as np
    import concourse.bacc as bacc
    from concourse.bass_utils import run_bass_kernel_spmd

    v = {k.split("_", 2)[2] if k.startswith("L0") else k: np.asarray(a) for k, a in inputs.items()}
    f = np.float32

    w_in = v["W_in"].reshape(2, NT, P, HK, P).transpose(1, 4, 0, 3, 2).reshape(NT, P, 2 * HK, P)
    w_dt = np.zeros((NT, P, P), f)
    w_dt[:, :R] = v["W_dt"].reshape(NT, P, R).transpose(0, 2, 1)
    w_dt[:, ONES_ROW] = v["b_dt"].reshape(NT, P)
    rec = np.concatenate([w_in, np.roll(w_dt, -1, axis=0)[:, :, None]], axis=2)
    rec = np.concatenate([rec, rec[:1]])
    experts = v["expert_w"].reshape(E, HK, P, H).transpose(0, 2, 1, 3)
    w_out = v["W_out"].T.reshape(2, HK, P, H).transpose(0, 2, 1, 3)
    arrays = {
        "x": v["hidden_states"].reshape(TOK, H),
        "win": rec,
        "wdt0": w_dt[0],
        "wx": v["W_x"].reshape(SSM, NT, P).transpose(2, 1, 0),
        "wring": np.concatenate([experts, w_out]),
        "gate_w": v["gate_w"].reshape(HK, P, E).transpose(1, 0, 2),
        "a_log": v["A_log"].reshape(NT * NR, CH, NG, NQ).transpose(2, 1, 0, 3).reshape(P, NT * UNITS),
        "conv_w": v["conv_w"].reshape(NT, P, K).transpose(1, 0, 2).reshape(P, NT * K),
        "conv_b": v["conv_b"].reshape(NT, P).T,
        "d_skip": v["D"].reshape(NT, P).T,
    }
    arrays = {k: np.ascontiguousarray(a) for k, a in arrays.items()}
    nc = bacc.Bacc("TRN2", target_bir_lowering=False, num_devices=1)
    aps = [nc.dram_tensor(k, a.shape, F32, kind="ExternalInput").ap() for k, a in arrays.items()]
    bc = nc.dram_tensor("bc_rows", (NCH, 2 * N, TC), F32, kind="Internal").ap()
    out = nc.dram_tensor("out", (TOK, H), F32, kind="ExternalOutput").ap()
    scan_moe(nc, *aps, bc, out)
    r = run_bass_kernel_spmd(nc, [arrays], core_ids=[0])
    return r.results[0]["out"].reshape(BATCH, SEQ, H)
```

```python
from contextlib import ExitStack

import concourse.bass as bass
from concourse import mybir

F32 = mybir.dt.float32
ALU = mybir.AluOpType
ACT = mybir.ActivationFunctionType
AX_X = mybir.AxisListType.X

P = 128
BATCH, SEQ, H = 2, 1024, 512
D_IN, N, K, R, E = 1024, 16, 4, 32, 8
TOK = BATCH * SEQ
TC = 512
NCH = TOK // TC
PER_ROW = SEQ // TC
NT = D_IN // P
HK = H // P
TT = TC // P
NG = 4
NQ = N // NG
CH = P // NG
NR = P // CH
UNITS = NR * NQ
SSM = R + 2 * N
ONES_ROW = 64
RMS_EPS, LN_EPS = 1e-6, 1e-5
LNEXP, SILU = "natural_log_exp_and_others", "silu_and_others"
DECAYS, DRIVES = 4, 2
REP = 16 * NG
PAIRS = NT // 2
START = 1


def scan_moe(nc, x, win, wdt0, wx, wring, gate_w, a_log, conv_w, conv_b, d_skip, bc_dram, out):
    with ExitStack() as ctx:
        def sb(name, *shape):
            return ctx.enter_context(nc.sbuf_tensor(name, [P, *shape], F32))

        def ps(name, *shape):
            return ctx.enter_context(nc.psum_tensor(name, [P, *shape], F32))

        def sem(name):
            return ctx.enter_context(nc.semaphore(name))

        xnT = sb("xnT", HK, TOK)
        decay = sb("decay", DECAYS * NQ, TC)
        drive = sb("drive", DRIVES * NQ, TC)
        w_ring = sb("w_ring", 2, HK, H)
        w_rec = sb("w_rec", 2 * HK + 1, P)
        w_dt0 = sb("w_dt0", P)
        w_x = sb("w_x", NT, SSM)
        w_gate = sb("w_gate", HK, E)
        xy = sb("xy", 2, NT, TC)
        gate = sb("gate", TC)
        moe = sb("moe", TT, H)
        rep = sb("rep", NR, 2, TC)
        b_all, c_all = sb("b_all", NQ, TC), sb("c_all", NQ, TC)
        x_pad = sb("x_pad", TC + K - 1)
        z = sb("z", TC)
        halo = sb("halo", NT, K - 1)
        t_e, t_l = sb("t_e", TC), sb("t_l", TC)
        dtu = sb("dtu", 2, TC)
        dt, u = dtu[:, 0, :], dtu[:, 1, :]
        dt_in = sb("dt_in", TC)
        part = sb("part", 2, H)
        y_t = sb("y_t", TC)
        res = sb("res", H)
        state = sb("state", NT * UNITS)
        a_neg = sb("a_neg", NT * UNITS)
        cw, cb, dsk = sb("cw", NT * K), sb("cb", NT), sb("dsk", NT)
        ident = sb("ident", P)
        stack = sb("stack", CH)
        w_e = sb("w_e", 16, E)
        spare = [rep[:, r, 0, :] for r in range(NR)]
        ident_i, stats, mv = spare[0][:, 0:P], spare[1][:, 0:96], spare[1][:, 96:128]
        stats, mv = stats.rearrange("p (k f) -> p k f", f=6), mv.rearrange("p (k f) -> p k f", f=2)
        nv, nl, nr, nt_, m1 = (spare[1][:, 128 + 16 * k:144 + 16 * k] for k in range(5))
        logit, rank, cmp_ = (spare[2][:, 128 * k:128 * (k + 1)].rearrange("p (t e) -> p t e", e=E) for k in range(3))
        ssm = sb("ssm", TT, SSM)
        sq = y_t[:, 0:TT * SSM].rearrange("p (t f) -> p t f", f=SSM)
        grp = sb("grp", TT, SSM // N)
        rv, rl, rr, rt = sb("rv", TT, 3), sb("rl", TT, 3), sb("rr", TT, 3), sb("rt", TT, 3)

        y_ps, f_ps = ps("y_ps", 2, TC), ps("f_ps", 2, TC)
        x_ps, g_ps, dt_ps, o_ps = ps("x_ps", TC), ps("g_ps", TC), ps("dt_ps", TC), ps("o_ps", TC)

        s_const = sem("s_const")
        s_x = [sem(f"s_x{g}") for g in range(NCH)]
        s_rec = sem("s_rec")
        s_wr = [sem(f"s_wr{s}") for s in range(2)]
        s_bc0 = sem("s_bc0")
        s_bc = sem("s_bc")
        s_rep = [sem(f"s_rep{r}") for r in range(NR)]
        s_res = sem("s_res")
        s_out = sem("s_out")
        id_zero, id_ok = sem("id_zero"), sem("id_ok")
        stack_ok = sem("stack_ok")
        a_exp, a_ok = sem("a_exp"), sem("a_ok")
        dve_link, act_link = sem("dve_link"), sem("act_link")
        ln_v, ln_r = sem("ln_v"), sem("ln_r")
        xn_ok = sem("xn_ok")
        tr_mm, tr_ev = sem("tr_mm"), sem("tr_ev")
        lg_mm = sem("lg_mm")
        lg_d, lg_e, we_ok = sem("lg_d"), sem("lg_e"), sem("we_ok")
        x_mm, x_ev = sem("x_mm"), sem("x_ev")
        conv_ok = sem("conv_ok")
        x_ok = sem("x_ok")
        g_mm, g_ok = sem("g_mm"), sem("g_ok")
        ssm_mm, ssm_v, ssm_r = sem("ssm_mm"), sem("ssm_v"), sem("ssm_r")
        ssm_ok, ssmT_mm, dtin_ok = sem("ssm_ok"), sem("ssmT_mm"), sem("dtin_ok")
        dt_mm, dt_ln, dt_ok = sem("dt_mm"), sem("dt_ln"), sem("dt_ok")
        decay_ok = sem("decay_ok")
        drive_ok = sem("drive_ok")
        scan_ok = sem("scan_ok")
        prod_ok = sem("prod_ok")
        sum_ok = sem("sum_ok")
        gated = sem("gated")
        f_mm = sem("f_mm")
        f_ev = sem("f_ev")
        f_add = sem("f_add")
        moe_ok = sem("moe_ok")
        moe_clear = sem("moe_clear")
        o_mm, o_mul, o_add = sem("o_mm"), sem("o_mul"), sem("o_add")
        chunk_ready = sem("chunk_ready")

        x_t = x.rearrange("(n p) h -> n p h", p=P)
        out_t = out.rearrange("(n p) h -> n p h", p=P)
        b_rows = R + N
        block = ctx.enter_context(nc.Block())

        def in_pairs(eng, chunk_body):
            with eng.Fori(0, PAIRS - 1) as pr:
                chunk_body(pr, False)
            chunk_body(PAIRS - 1, True)

        @block.sync
        def _(sp):
            for dst, src in ((a_neg[:, :], a_log), (w_x[:, :, :], wx), (w_gate[:, :, :], gate_w),
                             (cw[:, :], conv_w), (cb[:, :], conv_b), (dsk[:, :], d_skip), (w_dt0[:, :], wdt0)):
                sp.dma_start(dst, src).then_inc(s_const, 16)
            for g in range(NCH):
                for i in range(TT):
                    sp.dma_start(decay[:, g * TT + i, :], x_t[g * TT + i]).then_inc(s_x[g], 16)
            sp.dma_start(w_rec[:, :, :], win[0]).then_inc(s_rec, 16)
            sp.dma_start(w_ring[:, 0, :, :], wring[0]).then_inc(s_wr[0], 16)

            for t in range(NT):
                sp.wait_ge(x_mm, t + 1)
                sp.wait_ge(s_rec, 16 * t + 16)
                sp.dma_start(w_rec[:, :, :], win[t + 1]).then_inc(s_rec, 16)

            def spread(n):
                sp.wait_ge(dt_ok, n + 1)
                for r in range(NR):
                    if n:
                        sp.wait_ge(decay_ok, UNITS * (n - 1) + NQ * (r + 1))
                        sp.wait_ge(drive_ok, UNITS * (n - 1) + NQ * (r + 1))
                    for g in range(NG):
                        sp.dma_start(rep[CH * g:CH * (g + 1), r, :, :],
                                     dtu[CH * r:CH * (r + 1), :, :]).then_inc(s_rep[r], 16)

            def store(c, i):
                k = TT * c + i
                sp.wait_ge(o_add, k + 1)
                sp.dma_start(out_t[k], moe[:, i, :]).then_inc(s_out, 16)

            def load_residual(c, i):
                k = TT * c + i
                sp.wait_ge(o_add, k)
                sp.dma_start(res[:, :], x_t[k]).then_inc(s_res, 16)

            def finish(c):
                for i in range(TT):
                    load_residual(c, i)
                    if i >= 1:
                        store(c, i - 1)
                store(c, TT - 1)
                if c < NCH - 1:
                    sp.wait_ge(o_mm, TT * (c + 1))
                    sp.dma_start(w_ring[:, 0, :, :], wring[0]).then_inc(s_wr[0], 16)

            for c in range(NCH):
                sp.wait_ge(dtin_ok, c + 1)
                sp.dma_start(bc_dram[c], dt_in[R:R + 2 * N, :]).then_inc(s_bc0, 16)
                sp.wait_ge(s_bc0, 16 * (c + 1))
                if c:
                    sp.wait_ge(prod_ok, DRIVES + NR * NT * c)
                for k, dst in ((0, b_all), (N, c_all)):
                    for g in range(NG):
                        rows = bc_dram[c, k + NQ * g:k + NQ * (g + 1), :].rearrange("(o q) t -> o q t", o=1)
                        sp.dma_start(dst[CH * g:CH * (g + 1), :, :],
                                     rows.broadcast_to([CH, NQ, TC])).then_inc(s_bc, 16)
                spread(NT * c)
                if c:
                    finish(c - 1)

                for t in range(NT):
                    n = NT * c + t
                    sp.wait_ge(f_mm, TT * n)
                    sp.dma_start(w_ring[:, 1 - t % 2, :, :], wring[t + 1]).then_inc(s_wr[1 - t % 2], 16)
                    sp.wait_ge(g_mm, n + 1)
                    if c < NCH - 1:
                        sp.wait_ge(x_mm, NT * (c + 1) + t + 1)
                    if t < NT - 1:
                        sp.wait_ge(dt_mm, n + 2)
                    sp.wait_ge(s_rec, 16 * (NT + n + 1))
                    sp.dma_start(w_rec[:, :, :], win[t + 1]).then_inc(s_rec, 16)
                    if t < NT - 1:
                        spread(n + 1)
                sp.wait_ge(f_mm, TT * NT * (c + 1))
                sp.dma_start(w_ring[:, 1, :, :], wring[E + 1]).then_inc(s_wr[1], 16)
            finish(NCH - 1)
            sp.wait_ge(s_out, 16 * (TOK // P))

        @block.gpsimd
        def _(pool):
            pool.memset(ident_i[:, :], 0.0).then_inc(id_zero, 1)
            pool.wait_ge(id_zero, 1)
            pool.affine_select(out=ident[:, :], in_=ident_i[:, :], compare_op=ALU.not_equal, fill=1.0, base=0,
                               pattern=[[-1, P]], channel_multiplier=1).then_inc(id_ok, 1)
            pool.memset(moe[:, :, :], 0.0).then_inc(moe_clear, 1)
            pool.sem_inc(f_add, 2)

            for c in range(NCH):
                pool.wait_ge(s_bc, 16 * 2 * NG * (c + 1))
                pool.wait_ge(moe_clear, c + 1)

                def add_expert(k, i, c=c):
                    pool.wait_ge(f_ev, k + 3)
                    pool.wait_ge(f_add, k + 3 - TT if c else k + 2)
                    pool.tensor_tensor(moe[:, i, :], moe[:, i, :], part[:, i % 2, :], ALU.add).then_inc(f_add, 1)

                def drives(n, r):
                    pool.wait_ge(prod_ok, NR * n + r + 1)
                    pool.wait_ge(s_rep[r], REP * (n + 1))
                    for q in range(NQ):
                        pool.tensor_tensor(drive[:, NQ * (r % DRIVES) + q, :], rep[:, r, 1, :],
                                           b_all[:, q, :], ALU.mult).then_inc(drive_ok, 1)

                def body(pr, last, c=c):
                    for s in range(2):
                        n = NT * c + pr * 2 + s
                        drives(n, 1)
                        drives(n, 2)
                        add_expert(TT * n, 0)
                        drives(n, 3)
                        add_expert(TT * n + 1, 1)
                        add_expert(TT * n + 2, 2)
                        if not (last and s == 1):
                            drives(n + 1, 0)
                        add_expert(TT * n + 3, 3)
                drives(NT * c, 0)
                in_pairs(pool, body)

                for i in range(TT):
                    k = TT * c + i
                    pool.wait_ge(o_mul, k + 1)
                    pool.wait_ge(s_res, 16 * (k + 1))
                    pool.tensor_tensor(moe[:, i, :], moe[:, i, :], res[:, :], ALU.add).then_inc(o_add, 1)
                if c < NCH - 1:
                    pool.wait_ge(s_out, 16 * TT * (c + 1))
                    pool.memset(moe[:, :, :], 0.0).then_inc(moe_clear, 1)

        @block.scalar
        def _(act):
            links = [0]

            act.sem_inc(f_ev, 2)
            for s in (x_ev, x_ok, g_ok):
                act.sem_inc(s, START)
            act.preload_act_table_set(LNEXP)
            act.wait_ge(s_const, 16 * 7)
            act.activation(a_neg[:, :], a_neg[:, :], ACT.Exp).then_inc(a_exp, 1)

            def rsqrt_guess(src, tmp, dst, done, link_at):
                act.activation(tmp, src, ACT.Ln).then_inc(act_link, 1)
                act.wait_ge(act_link, link_at)
                act.activation(dst, tmp, ACT.Exp, scale=-0.5).then_inc(done, 1)

            act.wait_ge(ln_v, 1)
            links[0] += 1
            rsqrt_guess(nv, nl, nr, ln_r, links[0])
            for k in range(16):
                act.wait_ge(tr_mm, k + 1)
                act.copy(xnT[:, :, P * k:P * (k + 1)],
                         f_ps[:, k % 2, :].rearrange("p (k t) -> p k t", k=HK)).then_inc(tr_ev, 1)
            act.wait_ge(lg_d, 1)
            act.activation(w_e[:, :, :], logit[:, :, :], ACT.Exp).then_inc(lg_e, 1)

            def copy_x(c, t):
                j = NT * c + t
                act.wait_ge(x_mm, j + 1)
                act.wait_ge(conv_ok, START + j)
                act.copy(x_pad[:, K - 1:], x_ps[:, :]).then_inc(x_ev, 1)

            def silu_x(c, t):
                j = NT * c + t
                act.wait_ge(conv_ok, START + j + 1)
                act.activation(xy[:, c % 2, t, :], z[:, :], ACT.Silu).then_inc(x_ok, 1)

            act.preload_act_table_set(SILU)
            with act.Fori(0, NT) as t:
                copy_x(0, t)
                silu_x(0, t)
            act.preload_act_table_set(LNEXP)

            def step_sizes(n, links_at):
                act.wait_ge(dt_mm, n + 1)
                act.wait_ge(dt_ok, n)
                act.activation(t_e[:, :], dt_ps[:, :], ACT.Abs).then_inc(act_link, 1)
                act.wait_ge(act_link, links_at + 1)
                act.activation(t_e[:, :], t_e[:, :], ACT.Exp, scale=-1.0).then_inc(act_link, 1)
                act.wait_ge(act_link, links_at + 2)
                act.activation(t_l[:, :], t_e[:, :], ACT.Ln, bias=1.0).then_inc(dt_ln, 1)

            def decays(c, t, r):
                n = NT * c + t
                act.wait_ge(s_rep[r], REP * (n + 1))
                act.wait_ge(sum_ok, NR * n + r + 1)
                for q in range(NQ):
                    act.activation(decay[:, NQ * r + q, :], rep[:, r, 0, :], ACT.Exp,
                                   scale=a_neg[:, bass.ds(t * UNITS + r * NQ + q, 1)]).then_inc(decay_ok, 1)

            def weigh_expert(c, t, i):
                k = TT * (NT * c + t) + i
                act.wait_ge(f_mm, k + 1)
                act.wait_ge(f_add, k + 1)
                act.activation(part[:, i % 2, :], f_ps[:, i % 2, :], ACT.Copy,
                               scale=w_e[:, TT * c + i, bass.ds(t, 1)]).then_inc(f_ev, 1)

            act.wait_ge(a_ok, 1)
            act.wait_ge(we_ok, 1)
            for c in range(NCH):
                act.wait_ge(ssm_v, c + 1)
                links[0] += 1
                rsqrt_guess(rv[:, :, :], rl[:, :, :], rr[:, :, :], ssm_r, links[0])
                if c:
                    act.wait_ge(f_add, 2 + TT * NT * c)
                    act.preload_act_table_set(SILU)
                    act.activation(moe[:, :, :], moe[:, :, :], ACT.Silu).then_inc(moe_ok, 1)
                    act.preload_act_table_set(LNEXP)
                step_sizes(NT * c, links[0])
                links[0] += 2
                start = links[0]

                def body(pr, last, c=c, start=start):
                    for s in range(2):
                        t = pr * 2 + s
                        n = NT * c + t
                        decays(c, t, 1)
                        if not (last and s == 1):
                            step_sizes(n + 1, start + 2 * t)
                        decays(c, t, 2)
                        if c < NCH - 1:
                            copy_x(c + 1, t)
                        decays(c, t, 3)
                        weigh_expert(c, t, 0)
                        weigh_expert(c, t, 1)
                        act.preload_act_table_set(SILU)
                        act.wait_ge(g_mm, n + 1)
                        act.wait_ge(gated, START + n)
                        act.activation(gate[:, :], g_ps[:, :], ACT.Silu).then_inc(g_ok, 1)
                        if c < NCH - 1:
                            if c >= 1:
                                act.wait_ge(o_mm, TT * c)
                            silu_x(c + 1, t)
                        act.preload_act_table_set(LNEXP)
                        weigh_expert(c, t, 2)
                        weigh_expert(c, t, 3)
                        if not (last and s == 1):
                            decays(c, t + 1, 0)
                decays(c, 0, 0)
                in_pairs(act, body)
                links[0] += 2 * (NT - 1)
            act.wait_ge(f_add, 2 + TT * NT * NCH)
            act.preload_act_table_set(SILU)
            act.activation(moe[:, :, :], moe[:, :, :], ACT.Silu).then_inc(moe_ok, 1)

        @block.vector
        def _(dve):
            links = [0]

            def link(ins):
                links[0] += 1
                ins.then_inc(dve_link, 1)
                dve.wait_ge(dve_link, links[0])

            def newton(v, r, t):
                link(dve.tensor_tensor(t, v, r, ALU.mult))
                link(dve.tensor_tensor(t, t, r, ALU.mult))
                link(dve.tensor_scalar(t, t, -0.5, 1.5, ALU.mult, ALU.add))
                link(dve.tensor_tensor(r, r, t, ALU.mult))

            dve.sem_inc(prod_ok, DRIVES)
            for s in (conv_ok, gated):
                dve.sem_inc(s, START)
            dve.memset(dt_in[:, :], 1.0).then_inc(dve_link, 1)
            dve.memset(halo[:, :, :], 0.0).then_inc(dve_link, 1)
            links[0] += 2
            for g in range(NCH):
                dve.wait_ge(s_x[g], 16 * TT)
                for i in range(TT):
                    link_last = dve.bn_stats(stats[:, g * TT + i, :], decay[:, g * TT + i, :])
                    link_last.then_inc(dve_link, 1)
                    links[0] += 1
            dve.wait_ge(dve_link, links[0])
            for k in range(16):
                dve.bn_aggr(mv[:, k, :], stats[:, k, :]).then_inc(dve_link, 1)
                links[0] += 1
            dve.wait_ge(dve_link, links[0])
            link(dve.tensor_scalar(nv, mv[:, :, 1], LN_EPS, None, ALU.add))
            dve.sem_inc(ln_v, 1)
            dve.wait_ge(ln_r, 1)
            newton(nv, nr, nt_)
            for k in range(16):
                dve.tensor_scalar(decay[:, k, :], decay[:, k, :], mv[:, k, 0:1], nr[:, k:k + 1],
                                  ALU.subtract, ALU.mult).then_inc(xn_ok, 1)
            dve.wait_ge(id_ok, 1)
            link(dve.tensor_reduce(stack[:, :], ident[:, :].rearrange("p (g c) -> p c g", g=NG), AX_X, ALU.add))
            dve.sem_inc(stack_ok, 1)
            dve.wait_ge(a_exp, 1)
            dve.tensor_scalar(a_neg[:, :], a_neg[:, :], -1.0, None, ALU.mult).then_inc(a_ok, 1)

            dve.wait_ge(lg_mm, 1)
            link(dve.tensor_copy(logit[:, :, :], o_ps[:, 0:16 * E].rearrange("p (t e) -> p t e", e=E)))
            link(dve.tensor_reduce(m1, logit[:, :, :], AX_X, ALU.max))
            link(dve.memset(rank[:, :, :], 0.0))
            for e in range(E):
                if e:
                    dve.tensor_tensor(cmp_[:, :, 0:e], logit[:, :, e:e + 1].broadcast_to([P, 16, e]),
                                      logit[:, :, 0:e], ALU.is_gt).then_inc(dve_link, 1)
                    links[0] += 1
                dve.tensor_tensor(cmp_[:, :, e:E], logit[:, :, e:e + 1].broadcast_to([P, 16, E - e]),
                                  logit[:, :, e:E], ALU.is_ge).then_inc(dve_link, 1)
                links[0] += 1
                dve.wait_ge(dve_link, links[0])
                link(dve.tensor_tensor(rank[:, :, :], rank[:, :, :], cmp_[:, :, :], ALU.add))
            link(dve.tensor_tensor(logit[:, :, :], logit[:, :, :],
                                   m1.rearrange("p (t o) -> p t o", o=1).broadcast_to([P, 16, E]),
                                   ALU.subtract))
            dve.sem_inc(lg_d, 1)
            link(dve.tensor_scalar(rank[:, :, :], rank[:, :, :], 2.0, None, ALU.is_le))
            dve.wait_ge(lg_e, 1)
            link(dve.tensor_tensor(w_e[:, :, :], w_e[:, :, :], rank[:, :, :], ALU.mult))
            link(dve.tensor_reduce(m1, w_e[:, :, :], AX_X, ALU.add))
            link(dve.reciprocal(m1, m1))
            dve.tensor_tensor(w_e[:, :, :], w_e[:, :, :],
                              m1.rearrange("p (t o) -> p t o", o=1).broadcast_to([P, 16, E]),
                              ALU.mult).then_inc(we_ok, 1)

            def convolve(c, t, at):
                j = NT * c + t
                dve.wait_ge(x_ev, START + j + 1)
                dve.tensor_scalar(x_pad[:, 0:K - 1], halo[:, t, :], 1.0, None, ALU.mult).then_inc(dve_link, 1)
                dve.wait_ge(dve_link, at + 1)
                dve.tensor_scalar(halo[:, t, :], x_pad[:, TC:TC + K - 1], 1.0, None, ALU.mult).then_inc(dve_link, 1)
                dve.wait_ge(x_ok, START + j)
                dve.tensor_scalar(z[:, :], x_pad[:, 0:TC], cw[:, bass.ds(t * K, 1)], cb[:, bass.ds(t, 1)],
                                  ALU.mult, ALU.add).then_inc(dve_link, 1)
                for k in range(1, K):
                    dve.wait_ge(dve_link, at + 2 + k)
                    last = dve.scalar_tensor_tensor(out=z[:, :], in0=x_pad[:, k:k + TC],
                                                    scalar=cw[:, bass.ds(t * K + k, 1)], in1=z[:, :],
                                                    op0=ALU.mult, op1=ALU.add)
                    last.then_inc(dve_link if k < K - 1 else conv_ok, 1)
            CONV_LINKS = K + 1

            dve.wait_ge(dve_link, links[0])
            with dve.Fori(0, NT) as t:
                convolve(0, t, links[0] + CONV_LINKS * t)
            links[0] += CONV_LINKS * NT

            def step_sizes(c, t, spread, tiles, at):
                n = NT * c + t
                dve.wait_ge(dt_ln, n + 1)
                dve.wait_ge(gated, START + tiles)
                dve.tensor_scalar(y_t[:, :], t_e[:, :], 1.0, -1.0, ALU.add, ALU.add).then_inc(dve_link, 1)
                dve.wait_ge(dve_link, at + 1)
                dve.tensor_tensor(t_e[:, :], t_e[:, :], y_t[:, :], ALU.subtract).then_inc(dve_link, 1)
                dve.wait_ge(dve_link, at + 2)
                dve.tensor_tensor(t_l[:, :], t_l[:, :], t_e[:, :], ALU.add).then_inc(dve_link, 1)
                dve.wait_ge(dve_link, at + 3)
                if spread is not None:
                    for r in range(NR):
                        dve.wait_ge(s_rep[r], REP * spread)
                dve.scalar_tensor_tensor(out=dt[:, :], in0=dt_ps[:, :], scalar=0.0, in1=t_l[:, :],
                                         op0=ALU.max, op1=ALU.add).then_inc(dve_link, 1)
                dve.wait_ge(dve_link, at + 4)
                dve.wait_ge(x_ok, START + NT * (c + 1))
                dve.tensor_tensor(u[:, :], dt[:, :], xy[:, c % 2, t, :], ALU.mult).then_inc(dt_ok, 1)
            DT_LINKS = 4

            def quad(c, t, r):
                n = NT * c + t
                m = NR * n + r
                d0, u0 = NQ * r, NQ * (r % DRIVES)
                for q in range(NQ):
                    dve.wait_ge(decay_ok, UNITS * n + NQ * r + q + 1)
                    dve.wait_ge(drive_ok, UNITS * n + NQ * r + q + 1)
                    dve.tensor_tensor_scan(drive[:, u0 + q, :], decay[:, d0 + q, :], drive[:, u0 + q, :],
                                           state[:, bass.ds(t * UNITS + r * NQ + q, 1)],
                                           ALU.mult, ALU.add).then_inc(scan_ok, 1)
                dve.wait_ge(scan_ok, NQ * (m + 1))
                dve.tensor_scalar(state[:, bass.ds(t * UNITS + r * NQ, NQ)], drive[:, u0:u0 + NQ, TC - 1], 1.0, None,
                                  ALU.mult).then_inc(dve_link, 1)
                dve.tensor_tensor(decay[:, d0:d0 + NQ, :], drive[:, u0:u0 + NQ, :], c_all[:, :, :],
                                  ALU.mult).then_inc(prod_ok, 1)

            def gate_tile(c, t, s, at):
                n = NT * c + t
                dve.wait_ge(sum_ok, DECAYS + NR * (n + 1))
                dve.wait_ge(gated, START + n)
                dve.scalar_tensor_tensor(out=y_t[:, :], in0=xy[:, c % 2, t, :], scalar=dsk[:, bass.ds(t, 1)],
                                         in1=y_ps[:, s, :], op0=ALU.mult, op1=ALU.add).then_inc(dve_link, 1)
                dve.wait_ge(dve_link, at + 1)
                dve.wait_ge(g_ok, START + n + 1)
                dve.tensor_tensor(xy[:, c % 2, t, :], y_t[:, :], gate[:, :], ALU.mult).then_inc(gated, 1)

            def out_tile(c, i):
                k = TT * c + i
                dve.wait_ge(o_mm, k + 1)
                dve.wait_ge(moe_ok, c + 1)
                dve.tensor_tensor(moe[:, i, :], o_ps[:, :], moe[:, i, :], ALU.mult).then_inc(o_mul, 1)

            for c in range(NCH):
                dve.wait_ge(ssm_mm, c + 1)
                flat = "p t f -> p (t f)"
                link(dve.tensor_copy(ssm[:, :, :].rearrange(flat), x_ps[:, 0:TT * SSM]))
                link(dve.tensor_tensor(sq[:, :, :], ssm[:, :, :], ssm[:, :, :], ALU.mult))
                link(dve.tensor_reduce(grp[:, :, :].rearrange(flat),
                                       sq[:, :, :].rearrange("p t (g f) -> p (t g) f", f=N), AX_X, ALU.add))
                link(dve.tensor_tensor(rv[:, :, 0], grp[:, :, 0], grp[:, :, 1], ALU.add))
                link(dve.tensor_scalar(rv[:, :, 0], rv[:, :, 0], 1.0 / R, RMS_EPS, ALU.mult, ALU.add))
                link(dve.tensor_scalar(rv[:, :, 1:3], grp[:, :, 2:4], 1.0 / N, RMS_EPS, ALU.mult, ALU.add))
                dve.sem_inc(ssm_v, 1)
                dve.wait_ge(ssm_r, c + 1)
                newton(rv[:, :, :].rearrange(flat), rr[:, :, :].rearrange(flat), rt[:, :, :].rearrange(flat))
                link(dve.tensor_tensor(ssm[:, :, 0:R], ssm[:, :, 0:R],
                                       rr[:, :, 0:1].broadcast_to([P, TT, R]), ALU.mult))
                for k in range(2):
                    lo = R + N * k
                    link(dve.tensor_tensor(ssm[:, :, lo:lo + N], ssm[:, :, lo:lo + N],
                                           rr[:, :, k + 1:k + 2].broadcast_to([P, TT, N]), ALU.mult))
                dve.sem_inc(ssm_ok, 1)
                if c:
                    out_tile(c - 1, 0)
                dve.wait_ge(ssmT_mm, c + 1)
                if c:
                    dve.wait_ge(s_bc0, 16 * c)
                dve.tensor_copy(dt_in[0:SSM, :], dt_ps[0:SSM, :]).then_inc(dtin_ok, 1)
                if c:
                    out_tile(c - 1, 1)
                if c % PER_ROW == 0:
                    link(dve.memset(state[:, :], 0.0))
                if (c + 1) % PER_ROW == 0:
                    link(dve.memset(halo[:, :, :], 0.0))
                step_sizes(c, 0, NT * c if c else None, NT * c, links[0])
                links[0] += DT_LINKS
                if c:
                    out_tile(c - 1, 2)
                    out_tile(c - 1, 3)
                dve.wait_ge(s_bc, 16 * 2 * NG * (c + 1))

                conv = CONV_LINKS if c < NCH - 1 else 0
                per_pair = 2 * (NR + DT_LINKS + conv + 1)
                start = links[0]

                def body(pr, last, c=c, conv=conv, start=start, per_pair=per_pair):
                    at = start + pr * per_pair
                    for s in range(2):
                        t = pr * 2 + s
                        quad(c, t, 0)
                        at = at + 1
                        if s == 1:
                            gate_tile(c, t - 1, 0, at)
                            at = at + 1
                        quad(c, t, 1)
                        at = at + 1
                        if not (last and s == 1):
                            step_sizes(c, t + 1, NT * c + t + 1, NT * c + pr * 2 + s, at)
                            at = at + DT_LINKS
                        if conv:
                            convolve(c + 1, t, at)
                            at = at + conv
                        quad(c, t, 2)
                        quad(c, t, 3)
                        at = at + 2
                    gate_tile(c, t, 1, at)
                in_pairs(dve, body)
                links[0] = start + per_pair * PAIRS - DT_LINKS
            for i in range(TT):
                out_tile(NCH - 1, i)

        @block.tensor
        def _(pe):
            pe.sem_inc(sum_ok, DECAYS)
            pe.wait_ge(id_ok, 1)
            for k in range(16):
                pe.wait_ge(xn_ok, k + 1)
                if k >= 2:
                    pe.wait_ge(tr_ev, k - 1)
                for h in range(HK):
                    last = pe.transpose(f_ps[:, k % 2, P * h:P * (h + 1)], decay[:, k, P * h:P * (h + 1)], ident[:, :])
                last.then_inc(tr_mm, 1)
            pe.wait_ge(s_const, 16 * 7)
            pe.wait_ge(tr_ev, 16)
            for k in range(16):
                for h in range(HK):
                    last = pe.matmul(o_ps[:, E * k:E * (k + 1)], xnT[:, h, P * k:P * (k + 1)], w_gate[:, h, :],
                                     start=(h == 0), stop=(h == HK - 1))
            last.then_inc(lg_mm, 1)

            def project_x(c, t):
                j = NT * c + t
                pe.wait_ge(x_ev, START + j)
                for h in range(HK):
                    last = pe.matmul(x_ps[:, :], w_rec[:, h, :], xnT[:, h, TC * c:TC * (c + 1)],
                                     start=(h == 0), stop=(h == HK - 1))
                last.then_inc(x_mm, 1)

            with pe.Fori(0, NT) as t:
                pe.wait_ge(s_rec, 16 * (t + 1))
                project_x(0, t)

            def step_sizes(n, w):
                pe.wait_ge(dt_ok, n)
                pe.matmul(dt_ps[:, :], w, dt_in[:, :], start=True, stop=True).then_inc(dt_mm, 1)

            def out_tile(c, i):
                k = TT * c + i
                if k >= 1:
                    pe.wait_ge(o_mul, k)
                if i == 0:
                    pe.wait_ge(gated, START + NT * (c + 1))
                for t in range(NT):
                    if i == 0 and t % HK == 0:
                        pe.wait_ge(s_wr[t // HK], 16 * (5 * c + 5))
                    last = pe.matmul(o_ps[:, :], xy[:, c % 2, t, P * i:P * (i + 1)], w_ring[:, t // HK, t % HK, :],
                                     start=(t == 0), stop=(t == NT - 1))
                last.then_inc(o_mm, 1)

            def expert(c, t, pr, s, i):
                k = TT * (NT * c + t) + i
                if i == 0:
                    pe.wait_ge(s_wr[s], 16 * (5 * c + pr + 1))
                pe.wait_ge(f_ev, k + 1)
                for h in range(HK):
                    lo = TC * c + P * i
                    last = pe.matmul(f_ps[:, i % 2, :], xnT[:, h, lo:lo + P], w_ring[:, s, h, :],
                                     start=(h == 0), stop=(h == HK - 1))
                last.then_inc(f_mm, 1)

            def sum_states(c, t, s, r):
                m = NR * (NT * c + t) + r
                if r == 0:
                    pe.wait_ge(gated, START + NT * c + t - s)
                pe.wait_ge(prod_ok, DRIVES + m + 1)
                for q in range(NQ):
                    last = pe.matmul(y_ps[CH * r:CH * (r + 1), s, :], stack[:, :], decay[:, NQ * r + q, :],
                                     start=(q == 0), stop=(q == NQ - 1))
                last.then_inc(sum_ok, 1)

            pe.wait_ge(stack_ok, 1)
            for c in range(NCH):
                pe.wait_ge(x_ok, START + NT * (c + 1))
                pe.wait_ge(x_ev, START + NT * (c + 1))
                for i in range(TT):
                    for t in range(NT):
                        last = pe.matmul(x_ps[:, SSM * i:SSM * (i + 1)], xy[:, c % 2, t, P * i:P * (i + 1)],
                                         w_x[:, t, :], start=(t == 0), stop=(t == NT - 1))
                last.then_inc(ssm_mm, 1)
                if c:
                    out_tile(c - 1, 0)
                pe.wait_ge(ssm_ok, c + 1)
                pe.wait_ge(dt_ok, NT * c)
                for i in range(TT):
                    last = pe.transpose(dt_ps[0:SSM, P * i:P * (i + 1)], ssm[:, i, :], ident[:, :])
                last.then_inc(ssmT_mm, 1)
                if c:
                    out_tile(c - 1, 1)
                pe.wait_ge(dtin_ok, c + 1)
                step_sizes(NT * c, w_dt0[:, :])
                if c:
                    out_tile(c - 1, 2)
                    out_tile(c - 1, 3)

                def body(pr, last, c=c):
                    for s in range(2):
                        t = pr * 2 + s
                        n = NT * c + t
                        pe.wait_ge(s_rec, 16 * (NT + n + 1))
                        if not (last and s == 1):
                            step_sizes(n + 1, w_rec[:, 2 * HK, :])
                        if c < NCH - 1:
                            project_x(c + 1, t)
                        pe.wait_ge(g_ok, START + n)
                        for h in range(HK):
                            mm = pe.matmul(g_ps[:, :], w_rec[:, HK + h, :], xnT[:, h, TC * c:TC * (c + 1)],
                                           start=(h == 0), stop=(h == HK - 1))
                        mm.then_inc(g_mm, 1)
                        expert(c, t, pr, s, 0)
                        sum_states(c, t, s, 0)
                        expert(c, t, pr, s, 1)
                        sum_states(c, t, s, 1)
                        expert(c, t, pr, s, 2)
                        expert(c, t, pr, s, 3)
                        sum_states(c, t, s, 2)
                        sum_states(c, t, s, 3)
                in_pairs(pe, body)
            for i in range(TT):
                out_tile(NCH - 1, i)


def kernel(**inputs):
    import numpy as np
    import concourse.bacc as bacc
    from concourse.bass_utils import run_bass_kernel_spmd

    v = {k.split("_", 2)[2] if k.startswith("L0") else k: np.asarray(a) for k, a in inputs.items()}
    f = np.float32

    w_in = v["W_in"].reshape(2, NT, P, HK, P).transpose(1, 4, 0, 3, 2).reshape(NT, P, 2 * HK, P)
    w_dt = np.zeros((NT, P, P), f)
    w_dt[:, :R] = v["W_dt"].reshape(NT, P, R).transpose(0, 2, 1)
    w_dt[:, ONES_ROW] = v["b_dt"].reshape(NT, P)
    rec = np.concatenate([w_in, np.roll(w_dt, -1, axis=0)[:, :, None]], axis=2)
    rec = np.concatenate([rec, rec[:1]])
    experts = v["expert_w"].reshape(E, HK, P, H).transpose(0, 2, 1, 3)
    w_out = v["W_out"].T.reshape(2, HK, P, H).transpose(0, 2, 1, 3)
    arrays = {
        "x": v["hidden_states"].reshape(TOK, H),
        "win": rec,
        "wdt0": w_dt[0],
        "wx": v["W_x"].reshape(SSM, NT, P).transpose(2, 1, 0),
        "wring": np.concatenate([experts, w_out]),
        "gate_w": v["gate_w"].reshape(HK, P, E).transpose(1, 0, 2),
        "a_log": v["A_log"].reshape(NT * NR, CH, NG, NQ).transpose(2, 1, 0, 3).reshape(P, NT * UNITS),
        "conv_w": v["conv_w"].reshape(NT, P, K).transpose(1, 0, 2).reshape(P, NT * K),
        "conv_b": v["conv_b"].reshape(NT, P).T,
        "d_skip": v["D"].reshape(NT, P).T,
    }
    arrays = {k: np.ascontiguousarray(a) for k, a in arrays.items()}
    nc = bacc.Bacc("TRN2", target_bir_lowering=False, num_devices=1)
    aps = [nc.dram_tensor(k, a.shape, F32, kind="ExternalInput").ap() for k, a in arrays.items()]
    bc = nc.dram_tensor("bc_rows", (NCH, 2 * N, TC), F32, kind="Internal").ap()
    out = nc.dram_tensor("out", (TOK, H), F32, kind="ExternalOutput").ap()
    scan_moe(nc, *aps, bc, out)
    r = run_bass_kernel_spmd(nc, [arrays], core_ids=[0])
    return r.results[0]["out"].reshape(BATCH, SEQ, H)
```

```python
from contextlib import ExitStack

import concourse.bass as bass
from concourse import mybir

F32 = mybir.dt.float32
I32 = mybir.dt.int32
ALU = mybir.AluOpType
ACT = mybir.ActivationFunctionType
AX_X = mybir.AxisListType.X

P = 128
BATCH, SEQ, H = 2, 1024, 512
D_IN, N, K, R, E = 1024, 16, 4, 32, 8
TOK = BATCH * SEQ
TC = 512
NCH = TOK // TC
PER_ROW = SEQ // TC
NT = D_IN // P
HK = H // P
TT = TC // P
NG = 4
NQ = N // NG
CH = P // NG
NR = P // CH
UNITS = NR * NQ
SSM = R + 2 * N
ONES_ROW = 64
RMS_EPS, LN_EPS = 1e-6, 1e-5
LNEXP, SILU = "natural_log_exp_and_others", "silu_and_others"
DECAYS, DRIVES = 4, 2
REP = 16 * NG
PAIRS = NT // 2
SLOTS = 2 * TC // P + E - 1
ROWS = SLOTS * P
START = 1


def is_zero(i):
    return isinstance(i, int) and i == 0


def scan_moe(nc, x, win, wdt0, wx, wring, gate_w, means, a_log, conv_w, conv_b, d_skip,
             w_x7, token_ids, route_consts, bc_dram, xn_rows, order, slot_rows, out):
    with ExitStack() as ctx:
        def sb(name, *shape, dtype=F32):
            return ctx.enter_context(nc.sbuf_tensor(name, [P, *shape], dtype))

        def ps(name, *shape):
            return ctx.enter_context(nc.psum_tensor(name, [P, *shape], F32))

        def sem(name):
            return ctx.enter_context(nc.semaphore(name))

        xnT = sb("xnT", HK, TOK)
        decay = sb("decay", DECAYS * NQ, TC)
        drive = sb("drive", DRIVES * NQ, TC)
        w_ring = sb("w_ring", 2, HK, H)
        w_rec = sb("w_rec", 2 * HK + 2, P)
        w_dt0 = sb("w_dt0", P)
        w_x_last = sb("w_x_last", SSM)
        w_gate = sb("w_gate", HK, CH)
        mean_w = sb("mean_w", SSM)
        eps = sb("eps", 1)
        xy = sb("xy", 2, NT, TC)
        gate = sb("gate", TC)
        moe = sb("moe", TT, H)
        rep = sb("rep", NR, 2, TC)
        b_all, c_all = sb("b_all", NQ, TC), sb("c_all", NQ, TC)
        x_pad = sb("x_pad", TC + K - 1)
        z = sb("z", TC)
        halo = sb("halo", NT, K - 1)
        t_e, t_l = sb("t_e", TC), sb("t_l", TC)
        dtu = sb("dtu", 2, TC)
        dt, u = dtu[:, 0, :], dtu[:, 1, :]
        dt_in = sb("dt_in", TC)
        x_slot = sb("x_slot", H)
        xT_slot = sb("xT_slot", HK, P)
        y_slot = sb("y_slot", H)
        y_t = sb("y_t", TC)
        res = sb("res", H)
        state = sb("state", NT * UNITS)
        a_neg = sb("a_neg", NT * UNITS)
        cw, cb, dsk = sb("cw", NT * K), sb("cb", NT), sb("dsk", NT)
        ident = sb("ident", P)
        stack = sb("stack", CH)
        diag = sb("diag", P)
        tok_ids = sb("tok_ids", 16, dtype=I32)
        row1, row2 = sb("row1", 16, dtype=I32), sb("row2", 16, dtype=I32)
        p1, p2 = sb("p1", 16), sb("p2", 16)
        e_row = sb("e_row", NCH * SLOTS, dtype=I32)
        tok_now = sb("tok_now", 1, dtype=I32)
        slot_tok = sb("slot_tok", NCH * SLOTS, dtype=I32)
        spare = [moe[:, i, :] for i in range(TT)]
        ident_i, stats, mv = spare[0][:, 0:P], spare[1][:, 0:96], spare[1][:, 96:128]
        stats, mv = stats.rearrange("p (k f) -> p k f", f=6), mv.rearrange("p (k f) -> p k f", f=2)
        nv, nl, nr, nt_, m1 = (spare[1][:, 128 + 16 * k:144 + 16 * k] for k in range(5))
        logit, rank, cmp_ = (spare[2][:, 128 * k:128 * (k + 1)].rearrange("p (t e) -> p t e", e=E) for k in range(3))
        first, both, pos = (spare[0][:, 128 * k:128 * (k + 1)].rearrange("p (t e) -> p t e", e=E) for k in (1, 2, 3))
        ahead, sel = (spare[1][:, 128 * k:128 * (k + 1)].rearrange("p (t e) -> p t e", e=E) for k in (2, 3))
        count, tiles, tile0, tile1 = (spare[2][:, 384 + 32 * k:416 + 32 * k].rearrange("p (c e) -> p c e", e=E)
                                      for k in range(4))
        consts = spare[3][:, 0:2 * P + SLOTS]
        before, ones, slot_no = consts[:, 0:P], consts[:, P:2 * P], consts[:, 2 * P:2 * P + SLOTS]
        r1, r2, e1, e2, e_no = (spare[3][:, lo:lo + n] for lo, n in ((288, 16), (304, 16), (320, 16), (336, 16), (352, 60)))
        logit_T, past = y_t, y_t[:, 0:NCH * SLOTS * E].rearrange("p (c j e) -> p c j e", j=SLOTS, e=E)
        w_x = gate[:, :].rearrange("p (t f) -> p t f", f=SSM)
        second = [y_slot[:, :], x_slot[:, :], res[:, :], xT_slot[:, :, :].rearrange("p k m -> p (k m)")]
        x_w = drive

        y_ps, f_ps = ps("y_ps", 2, TC), ps("f_ps", 2, TC)
        x_ps, g_ps, dt_ps, o_ps = ps("x_ps", TC), ps("g_ps", TC), ps("dt_ps", TC), ps("o_ps", TC)

        def out_bank(c, i):
            if c < NCH - 1:
                return (o_ps[:, :], f_ps[:, 0, :], f_ps[:, 1, :], o_ps[:, :])[i]
            return (o_ps[:, :], x_ps[:, :], dt_ps[:, :], f_ps[:, 0, :])[i]

        def residual(c, i):
            return res[:, :] if c < NCH - 1 else b_all[:, i, :]

        s_const = sem("s_const")
        s_x = [sem(f"s_x{g}") for g in range(NCH)]
        s_xw = sem("s_xw")
        s_rec = sem("s_rec")
        s_wr = [sem(f"s_wr{s}") for s in range(2)]
        s_bc0 = sem("s_bc0")
        s_b, s_c = sem("s_b"), sem("s_c")
        s_rep = [sem(f"s_rep{r}") for r in range(NR)]
        s_wo = [sem("s_wo0"), sem("s_wo1")]
        s_res = sem("s_res")
        s_out = sem("s_out")
        id_zero, id_ok = sem("id_zero"), sem("id_ok")
        stack_ok = sem("stack_ok")
        a_exp, a_ok = sem("a_exp"), sem("a_ok")
        dve_link, act_link = sem("dve_link"), sem("act_link")
        ln_v, ln_r = sem("ln_v"), sem("ln_r")
        xn_ok = sem("xn_ok")
        tr_mm, tr_ev = sem("tr_mm"), sem("tr_ev")
        lgT_mm, lgT_ok, lg_mm = sem("lgT_mm"), sem("lgT_ok"), sem("lg_mm")
        lg_d, lg_e = sem("lg_d"), sem("lg_e")
        pick_ok, pos_mm = sem("pick_ok"), sem("pos_mm")
        slot_ok, prob_ok = sem("slot_ok"), sem("prob_ok")
        tok_zero = sem("tok_zero")
        s_zero, s_xn = sem("s_zero"), sem("s_xn")
        s_scat, s_list = sem("s_scat"), sem("s_list")
        tok_ok, tok_seen = sem("tok_ok"), sem("tok_seen")
        s_gx = sem("s_gx")
        xt_mm, xt_ev = sem("xt_mm"), sem("xt_ev")
        s_ys = sem("s_ys")
        s_pair = [sem(f"s_pair{i}") for i in range(TT)]
        scaled, comb_ok = sem("scaled"), sem("comb_ok")
        diag_ok, skip_mm = sem("diag_ok"), sem("skip_mm")
        x_mm, x_ev = sem("x_mm"), sem("x_ev")
        pad_ok, tap_ok, halo_ok = sem("pad_ok"), sem("tap_ok"), sem("halo_ok")
        conv_ok = sem("conv_ok")
        x_ok = sem("x_ok")
        g_mm, g_ok = sem("g_mm"), sem("g_ok")
        ssm_mm, sq_ok, mean_mm = sem("ssm_mm"), sem("sq_ok"), sem("mean_mm")
        ssm_r, dtin_ok = sem("ssm_r"), sem("dtin_ok")
        dt_mm, dt_ln, dt_ok = sem("dt_mm"), sem("dt_ln"), sem("dt_ok")
        decay_ok = sem("decay_ok")
        drive0_ok = sem("drive0_ok")
        drive_ok = sem("drive_ok")
        scan_ok = sem("scan_ok")
        prod_ok = sem("prod_ok")
        sum_ok = sem("sum_ok")
        gated = sem("gated")
        f_mm, f_ev = sem("f_mm"), sem("f_ev")
        moe_ok = sem("moe_ok")
        o_mm, o_mul, o_add = sem("o_mm"), sem("o_mul"), sem("o_add")

        x_t = x.rearrange("(n p) h -> n p h", p=P)
        out_t = out.rearrange("(n p) h -> n p h", p=P)
        w_rows = wring.rearrange("e p k m -> (e p) k m")
        block = ctx.enter_context(nc.Block())

        def slots_of(c, t):
            ahead = c == NCH - 1 and not (isinstance(t, int) and t == 1)
            return 2 * t - 2 + ahead, 2 * t - 1 + ahead

        def in_pairs(eng, chunk_body):
            chunk_body(0, True, False)
            with eng.Fori(1, PAIRS - 1) as pr:
                chunk_body(pr, False, False)
            chunk_body(PAIRS - 1, False, True)

        @block.sync
        def _(sp):
            for i in range(TT):
                sp.dma_start(decay[:, i, :], x_t[i]).then_inc(s_x[0], 16)
            sp.dma_start(x_w[:, :, :].rearrange("p t (k m) -> p t k m", k=HK),
                         win[0:NT, :, 0:HK, :].rearrange("t p k m -> p t k m")).then_inc(s_xw, 16)
            for dst, src in ((a_neg[:, :], a_log), (w_x[:, :, :], wx), (w_gate[:, :, :], gate_w),
                             (cw[:, :], conv_w), (cb[:, :], conv_b), (dsk[:, :], d_skip), (w_dt0[:, :], wdt0),
                             (mean_w[0:SSM, :], means), (w_x_last[:, :], w_x7), (tok_ids[:, :], token_ids),
                             (consts[:, :], route_consts)):
                sp.dma_start(dst, src).then_inc(s_const, 16)
            for g in range(1, NCH):
                for i in range(TT):
                    sp.dma_start(decay[:, g * TT + i, :], x_t[g * TT + i]).then_inc(s_x[g], 16)
            sp.dma_start(w_rec[:, :, :], win[0]).then_inc(s_rec, 16)
            sp.wait_ge(tok_zero, 1)
            for c in range(NCH):
                sp.dma_start(order[c].rearrange("(p j) o -> p (j o)", p=P),
                             slot_tok[:, SLOTS * c:SLOTS * (c + 1)]).then_inc(s_zero, 16)
            for k in range(16):
                sp.wait_ge(xn_ok, k + 1)
                sp.dma_start(xn_rows[P * k:P * (k + 1), :], decay[:, k, :]).then_inc(s_xn, 16)

            def load_order(c):
                sp.wait_ge(s_scat, 16 * 2 * TT * (c + 1))
                sp.dma_start(slot_tok[:, SLOTS * c:SLOTS * (c + 1)],
                             order[c].rearrange("(j p) o -> p (j o)", p=P),
                             allow_slow_non_contiguous=True).then_inc(s_list, 16)

            def load_expert(c, j):
                row = sp.value_load(e_row[0:1, SLOTS * c + j:SLOTS * c + j + 1], min_val=0, max_val=P * (E - 1))
                sp.dma_start(w_ring[:, j % 2, :, :], w_rows[bass.ds(row, P), :, :]).then_inc(s_wr[j % 2], 16)

            def load_w_out(slot, half):
                sp.dma_start(w_ring[:, slot, :, :], wring[E + half]).then_inc(s_wr[slot], 16)

            def store_slot(c, j):
                m = SLOTS * c + j
                sp.wait_ge(f_ev, m + 1)
                sp.dma_start(slot_rows[c][P * j:P * (j + 1), :], y_slot[:, :]).then_inc(s_ys, 16)

            def spread(n, lo=0, hi=NR):
                sp.wait_ge(dt_ok, n + 1)
                for r in range(lo, hi):
                    if n:
                        sp.wait_ge(decay_ok, UNITS * (n - 1) + NQ * (r + 1))
                        sp.wait_ge(drive_ok, UNITS * (n - 1) + NQ * (r + 1))
                    for g in range(NG):
                        sp.dma_start(rep[CH * g:CH * (g + 1), r, :, :],
                                     dtu[CH * r:CH * (r + 1), :, :]).then_inc(s_rep[r], 16)

            def spread_rows(c, k, dst, done):
                for g in range(NG):
                    rows = bc_dram[c, k + NQ * g:k + NQ * (g + 1), :].rearrange("(o q) t -> o q t", o=1)
                    sp.dma_start(dst[CH * g:CH * (g + 1), :, :], rows.broadcast_to([CH, NQ, TC])).then_inc(done, 16)

            def store(c, i):
                k = TT * c + i
                sp.wait_ge(o_add, k + 1)
                sp.dma_start(out_t[k], moe[:, i, :]).then_inc(s_out, 16)

            def load_residual(c, i):
                k = TT * c + i
                if c < NCH - 1:
                    sp.wait_ge(comb_ok, TT * (c + 1))
                    if k:
                        sp.wait_ge(o_add, k)
                sp.dma_start(residual(c, i), x_t[k]).then_inc(s_res, 16)

            def finish_head(c):
                for i in range(TT):
                    load_residual(c, i)
                    if i >= 1:
                        store(c, i - 1)

            for c in range(NCH):
                sp.wait_ge(dtin_ok, c + 1)
                sp.dma_start(bc_dram[c], dt_in[R:R + 2 * N, :]).then_inc(s_bc0, 16)
                sp.wait_ge(s_bc0, 16 * (c + 1))
                if c:
                    sp.wait_ge(drive_ok, UNITS * NT * c)
                    sp.wait_ge(drive0_ok, c)
                spread_rows(c, 0, b_all, s_b)
                if c:
                    store_slot(c - 1, SLOTS - 2)
                spread(NT * c, 0, 2)
                if c:
                    sp.wait_ge(prod_ok, DRIVES + NR * NT * c)
                spread_rows(c, N, c_all, s_c)
                if c:
                    load_w_out(1, 0)
                    store_slot(c - 1, SLOTS - 1)
                spread(NT * c, 2, NR)
                if c:
                    load_w_out(0, 1)
                    load_order(c)
                else:
                    load_order(0)
                    for j in range(2):
                        load_expert(0, j)

                for t in range(NT):
                    n = NT * c + t
                    if c and t == 1:
                        store(c - 1, TT - 1)
                    if n < NT * NCH - 1:
                        sp.wait_ge(g_mm, n + 1)
                        if c < NCH - 1:
                            sp.wait_ge(x_mm, NT * (c + 1) + t + 1)
                        if t < NT - 1:
                            sp.wait_ge(dt_mm, n + 2)
                        sp.wait_ge(s_rec, 16 * (n + 1))
                        sp.dma_start(w_rec[:, :, :], win[t + 1]).then_inc(s_rec, 16)
                    if t < NT - 1:
                        spread(n + 1)
                    if t >= 1:
                        a, b = slots_of(c, t)
                        for j in (a, b, 2) if c == NCH - 1 and t == 1 else (a, b):
                            if j == SLOTS - 2 and c < NCH - 1:
                                break
                            store_slot(c, j)
                            if j + 2 < SLOTS:
                                load_expert(c, j + 2)
                    elif c:
                        finish_head(c - 1)
                        sp.wait_ge(o_mm, TT * c)
                        for j in range(2):
                            load_expert(c, j)
                    if c == NCH - 1 and t in (1, HK):
                        half = t // HK
                        sp.dma_start(xy[:, 1 - c % 2, HK * half:HK * (half + 1), :],
                                     wring[E + half]).then_inc(s_wo[half], 16)
            sp.wait_ge(drive_ok, UNITS * NT * NCH)
            for i in range(TT):
                load_residual(NCH - 1, i)
            for i in range(TT):
                store(NCH - 1, i)
            sp.wait_ge(s_out, 16 * (TOK // P))

        @block.gpsimd
        def _(pool):
            pool.memset(ident_i[:, :], 0.0).then_inc(id_zero, 1)
            pool.wait_ge(id_zero, 1)
            pool.affine_select(out=ident[:, :], in_=ident_i[:, :], compare_op=ALU.not_equal, fill=1.0, base=0,
                               pattern=[[-1, P]], channel_multiplier=1).then_inc(id_ok, 1)
            pool.memset(slot_tok[:, :], 0).then_inc(tok_zero, 1)

            def put_in_order(c):
                for k in range(TT * c, TT * (c + 1)):
                    for row in (row1, row2):
                        pool.indirect_dma_start(order[c][:, :], bass.IndirectOffsetOnAxis(ap=row[:, k:k + 1], axis=0),
                                                tok_ids[:, k:k + 1], None).then_inc(s_scat, 16)

            def gather_slot(c, j):
                m = SLOTS * c + j
                if c and is_zero(j):
                    pool.wait_ge(comb_ok, TT * c)
                if not (c == 0 and is_zero(j)):
                    pool.wait_ge(xt_mm, m)
                pool.wait_ge(s_list, 16 * (c + 1))
                if not (c == 0 and is_zero(j)):
                    pool.wait_ge(s_gx, 16 * m)
                pool.tensor_copy(tok_now[:, :], slot_tok[:, bass.ds(m, 1)]).then_inc(tok_ok, 1)
                pool.wait_ge(tok_ok, m + 1)
                pool.sem_inc(tok_seen, 1)
                pool.indirect_dma_start(x_slot[:, :], None, xn_rows[:, :],
                                        bass.IndirectOffsetOnAxis(ap=tok_now[:, 0:1], axis=0)).then_inc(s_gx, 16)

            def gather_pairs(c, lo=0, hi=TT):
                pool.wait_ge(s_ys, 16 * SLOTS * (c + 1))
                if c:
                    pool.wait_ge(s_out, 16 * TT * c)
                for i in range(lo, hi):
                    k = TT * c + i
                    for dst, row in ((moe[:, i, :], row1), (second[i], row2)):
                        pool.indirect_dma_start(dst, None, slot_rows[c][:, :],
                                                bass.IndirectOffsetOnAxis(ap=row[:, k:k + 1], axis=0)).then_inc(s_pair[i], 16)

            def drives(n, r):
                pool.wait_ge(prod_ok, NR * n + r + 1)
                pool.wait_ge(s_rep[r], REP * (n + 1))
                for q in range(NQ):
                    pool.tensor_tensor(drive[:, NQ * (r % DRIVES) + q, :], rep[:, r, 1, :],
                                       b_all[:, q, :], ALU.mult).then_inc(drive_ok, 1)

            def add_residual(c, i):
                k = TT * c + i
                pool.wait_ge(o_mul, k + 1)
                pool.wait_ge(s_res, 16 * (k + 1) if c < NCH - 1 else 16 * TT * NCH)
                pool.tensor_tensor(moe[:, i, :], moe[:, i, :], residual(c, i), ALU.add).then_inc(o_add, 1)

            pool.wait_ge(slot_ok, 1)
            pool.wait_ge(s_const, 16 * 11)
            pool.wait_ge(s_zero, 16 * NCH)
            put_in_order(0)
            pool.wait_ge(x_mm, NT)
            for c in range(NCH):
                pool.wait_ge(s_b, 16 * NG * (c + 1))

                def body(pr, first, last, c=c):
                    for s in range(2):
                        t = pr * 2 + s
                        n = NT * c + t
                        drives(n, 1)
                        if first and s == 0:
                            if c:
                                gather_pairs(c - 1, 0, 2)
                            drives(n, 2)
                            if c:
                                gather_pairs(c - 1, 2, TT)
                            drives(n, 3)
                            gather_slot(c, 0)
                            drives(n + 1, 0)
                            if c:
                                add_residual(c - 1, 0)
                                add_residual(c - 1, 1)
                            continue
                        if first and c:
                            add_residual(c - 1, 2)
                        b = slots_of(c, t)[1]
                        gather_slot(c, b)
                        drives(n, 2)
                        if first and c:
                            add_residual(c - 1, 3)
                        drives(n, 3)
                        end = last and s == 1
                        if not (end and c == NCH - 1):
                            gather_slot(c, b + 1)
                        if end and c < NCH - 1:
                            put_in_order(c + 1)
                        if not end:
                            drives(n + 1, 0)
                        if first and c == NCH - 1:
                            gather_slot(c, b + 2)

                pool.sem_inc(drive_ok, NQ)
                in_pairs(pool, body)
            gather_pairs(NCH - 1)
            for i in range(TT):
                add_residual(NCH - 1, i)

        @block.scalar
        def _(act):
            links = [0]

            for s in (x_ev, x_ok, g_ok):
                act.sem_inc(s, START)
            act.preload_act_table_set(LNEXP)

            def rsqrt_guess(src, tmp, dst, done, **bias):
                links[0] += 1
                act.activation(tmp, src, ACT.Ln, **bias).then_inc(act_link, 1)
                act.wait_ge(act_link, links[0])
                act.activation(dst, tmp, ACT.Exp, scale=-0.5).then_inc(done, 1)

            def copy_transposed(tiles):
                for k in tiles:
                    act.wait_ge(tr_mm, k + 1)
                    act.copy(xnT[:, :, P * k:P * (k + 1)],
                             f_ps[:, k % 2, :].rearrange("p (k t) -> p k t", k=HK)).then_inc(tr_ev, 1)

            def copy_x(c, t):
                j = NT * c + t
                act.wait_ge(conv_ok, START + j)
                act.activation(x_pad[:, 0:K - 1], halo[:, t, :], ACT.Copy).then_inc(pad_ok, 1)
                act.wait_ge(x_mm, j + 1)
                act.copy(x_pad[:, K - 1:], x_ps[:, :]).then_inc(x_ev, 1)
                act.wait_ge(pad_ok, j + 1)
                act.wait_ge(x_ev, START + j + 1)
                act.wait_ge(x_ok, START + j)
                act.activation(z[:, :], x_pad[:, 0:TC], ACT.Identity, scale=cw[:, bass.ds(t * K, 1)],
                               bias=cb[:, bass.ds(t, 1)]).then_inc(tap_ok, 1)
                act.activation(halo[:, t, :], x_pad[:, TC:TC + K - 1], ACT.Copy).then_inc(halo_ok, 1)

            def silu_x(c, t):
                j = NT * c + t
                act.wait_ge(conv_ok, START + j + 1)
                act.activation(xy[:, c % 2, t, :], z[:, :], ACT.Silu).then_inc(x_ok, 1)

            act.wait_ge(ln_v, 1)
            rsqrt_guess(nv[:, 0:TT], nl[:, 0:TT], nr[:, 0:TT], ln_r)
            act.wait_ge(s_const, 16 * 11)
            act.activation(a_neg[:, :], a_neg[:, :], ACT.Exp).then_inc(a_exp, 1)
            copy_transposed(range(TT))
            copy_x(0, 0)
            act.wait_ge(ln_v, 2)
            rsqrt_guess(nv[:, TT:], nl[:, TT:], nr[:, TT:], ln_r)

            act.preload_act_table_set(SILU)
            copy_transposed(range(TT, NCH * TT))
            silu_x(0, 0)
            copy_x(0, 1)
            silu_x(0, 1)
            act.wait_ge(lgT_mm, 1)
            act.copy(logit_T[:, :], g_ps[:, :]).then_inc(lgT_ok, 1)
            with act.Fori(2, NT) as t:
                copy_x(0, t)
                silu_x(0, t)
            act.preload_act_table_set(LNEXP)
            act.wait_ge(lg_d, 1)
            act.activation(logit[:, :, :], logit[:, :, :], ACT.Exp).then_inc(lg_e, 1)

            def step_sizes(n, links_at):
                act.wait_ge(dt_mm, n + 1)
                act.wait_ge(dt_ok, n)
                act.activation(t_e[:, :], dt_ps[:, :], ACT.Abs).then_inc(act_link, 1)
                act.wait_ge(act_link, links_at + 1)
                act.activation(t_e[:, :], t_e[:, :], ACT.Exp, scale=-1.0).then_inc(act_link, 1)
                act.wait_ge(act_link, links_at + 2)
                act.activation(t_l[:, :], t_e[:, :], ACT.Ln, bias=1.0).then_inc(dt_ln, 1)
                if not is_zero(n):
                    for r in range(NR):
                        act.wait_ge(s_rep[r], REP * n)
                act.activation(dt, t_e[:, :], ACT.Identity, bias=1.0).then_inc(dt_ln, 1)

            def decays(c, t, r):
                n = NT * c + t
                act.wait_ge(s_rep[r], REP * (n + 1))
                act.wait_ge(sum_ok, NR * n + r + 1)
                for q in range(NQ):
                    act.activation(decay[:, NQ * r + q, :], rep[:, r, 0, :], ACT.Exp,
                                   scale=a_neg[:, bass.ds(t * UNITS + r * NQ + q, 1)]).then_inc(decay_ok, 1)

            def copy_slot_T(c, j):
                m = SLOTS * c + j
                act.wait_ge(xt_mm, m + 1)
                if c and is_zero(j):
                    act.wait_ge(comb_ok, TT * c)
                if not (c == 0 and is_zero(j)):
                    act.wait_ge(f_mm, m)
                act.copy(xT_slot[:, :, :], f_ps[:, 0, :].rearrange("p (k t) -> p k t", k=HK)).then_inc(xt_ev, 1)

            def copy_slot_y(c, j):
                m = SLOTS * c + j
                act.wait_ge(f_mm, m + 1)
                if not (c == 0 and is_zero(j)):
                    act.wait_ge(s_ys, 16 * m)
                if c and is_zero(j):
                    act.wait_ge(comb_ok, TT * c)
                act.copy(y_slot[:, :], f_ps[:, 1, :]).then_inc(f_ev, 1)

            def diagonal(n, t):
                if not is_zero(n):
                    act.wait_ge(skip_mm, n)
                act.activation(diag[:, :], ident[:, :], ACT.Copy, scale=dsk[:, bass.ds(t, 1)]).then_inc(diag_ok, 1)

            def scale_first(c, lo=0, hi=TT):
                if c == 0:
                    act.wait_ge(prob_ok, 1)
                for i in range(lo, hi):
                    act.wait_ge(s_pair[i], 16 * 2 * (c + 1))
                    act.activation(moe[:, i, :], moe[:, i, :], ACT.Copy,
                                   scale=p1[:, TT * c + i:TT * c + i + 1]).then_inc(scaled, 1)

            def mid(c):
                act.wait_ge(ssm_mm, c + 1)
                if c:
                    act.wait_ge(dt_ok, NT * c)
                act.activation(t_e[0:SSM, :], o_ps[0:SSM, :], ACT.Square).then_inc(sq_ok, 1)
                act.wait_ge(mean_mm, c + 1)
                rsqrt_guess(dt_ps[0:SSM, :], t_l[0:SSM, :], t_l[0:SSM, :], ssm_r, bias=eps[0:SSM, 0:1])
                if c:
                    decays(c - 1, NT - 1, 3)
                    copy_slot_y(c - 1, SLOTS - 3)
                    copy_slot_T(c - 1, SLOTS - 2)
                step_sizes(NT * c, links[0])
                links[0] += 2
                if c:
                    copy_slot_y(c - 1, SLOTS - 2)
                    copy_slot_T(c - 1, SLOTS - 1)
                if c == 0:
                    act.wait_ge(a_ok, 1)
                    act.wait_ge(s_xn, 16 * 16)
                if c:
                    copy_slot_y(c - 1, SLOTS - 1)
                decays(c, 0, 0)

            def silu_moe(c, lo=0, hi=TT):
                act.wait_ge(comb_ok, TT * c + hi)
                act.activation(moe[:, lo:hi, :], moe[:, lo:hi, :], ACT.Silu).then_inc(moe_ok, hi - lo)

            mid(0)
            for c in range(NCH):
                start = links[0]

                def body(pr, first, last, c=c, start=start):
                    for s in range(2):
                        t = pr * 2 + s
                        n = NT * c + t
                        diagonal(n, t)
                        decays(c, t, 1)
                        late = first and c and c < NCH - 1
                        if not (last and s == 1):
                            step_sizes(n + 1, start + 2 * t)
                        if late and s == 1:
                            act.preload_act_table_set(SILU)
                            act.wait_ge(o_mm, TT * c)
                            silu_x(c + 1, 0)
                            act.preload_act_table_set(LNEXP)
                        mixing = not (first and s == 0)
                        a, b = slots_of(c, t)
                        end = last and s == 1
                        if c < NCH - 1:
                            copy_x(c + 1, t)
                        if mixing:
                            copy_slot_T(c, a)
                        decays(c, t, 2)
                        if last and c == NCH - 1:
                            copy_slot_y(c, a)
                            copy_slot_T(c, b)
                        if not (end and c < NCH - 1):
                            decays(c, t, 3)
                        if end and c == NCH - 1:
                            copy_slot_y(c, b)
                        elif mixing and not last:
                            copy_slot_y(c, a)
                            copy_slot_T(c, b)
                        elif mixing and not end and c < NCH - 1:
                            copy_slot_y(c, a)
                            copy_slot_T(c, b)
                        elif c and not mixing:
                            scale_first(c - 1)
                        if not end:
                            decays(c, t + 1, 0)
                        act.preload_act_table_set(SILU)
                        if c and not mixing:
                            silu_moe(c - 1)
                        if end and c < NCH - 1:
                            silu_x(c + 1, t)
                        act.wait_ge(g_mm, n + 1)
                        act.wait_ge(gated, START + n)
                        act.activation(gate[:, :], g_ps[:, :], ACT.Silu).then_inc(g_ok, 1)
                        if c < NCH - 1 and not end and not (late and s == 0):
                            silu_x(c + 1, t)
                        act.preload_act_table_set(LNEXP)
                        if mixing and not end:
                            copy_slot_y(c, b)
                        if mixing and first and c == NCH - 1:
                            copy_slot_T(c, 2)
                            copy_slot_y(c, 2)
                in_pairs(act, body)
                links[0] += 2 * (NT - 1)
                if c < NCH - 1:
                    mid(c + 1)
            scale_first(NCH - 1)
            act.preload_act_table_set(SILU)
            for i in range(TT):
                silu_moe(NCH - 1, i, i + 1)

        @block.vector
        def _(dve):
            links = [0]

            def link(ins):
                links[0] += 1
                ins.then_inc(dve_link, 1)
                dve.wait_ge(dve_link, links[0])

            def newton(v, r, t):
                link(dve.tensor_tensor(t, v, r, ALU.mult))
                link(dve.tensor_tensor(t, t, r, ALU.mult))
                link(dve.tensor_scalar(t, t, -0.5, 1.5, ALU.mult, ALU.add))
                link(dve.tensor_tensor(r, r, t, ALU.mult))

            dve.sem_inc(prod_ok, DRIVES)
            for s in (conv_ok, gated):
                dve.sem_inc(s, START)
            dve.memset(dt_in[:, :], 1.0).then_inc(dve_link, 1)
            dve.memset(halo[:, :, :], 0.0).then_inc(dve_link, 1)
            dve.memset(eps[:, :], RMS_EPS).then_inc(dve_link, 1)
            dve.memset(state[:, :], 0.0).then_inc(dve_link, 1)
            links[0] += 4

            def variances(chunks):
                for g in chunks:
                    dve.wait_ge(s_x[g], 16 * TT)
                    for k in range(g * TT, (g + 1) * TT):
                        dve.bn_stats(stats[:, k, :], decay[:, k, :]).then_inc(dve_link, 1)
                        links[0] += 1
                dve.wait_ge(dve_link, links[0])
                lo, hi = chunks[0] * TT, (chunks[-1] + 1) * TT
                for k in range(lo, hi):
                    dve.bn_aggr(mv[:, k, :], stats[:, k, :]).then_inc(dve_link, 1)
                    links[0] += 1
                dve.wait_ge(dve_link, links[0])
                dve.tensor_scalar(nv[:, lo:hi], mv[:, lo:hi, 1], LN_EPS, None, ALU.add).then_inc(ln_v, 1)

            def normalise(count, lo, hi):
                dve.wait_ge(ln_r, count)
                newton(nv[:, lo:hi], nr[:, lo:hi], nt_[:, lo:hi])
                for k in range(lo, hi):
                    dve.tensor_scalar(decay[:, k, :], decay[:, k, :], mv[:, k, 0:1], nr[:, k:k + 1],
                                      ALU.subtract, ALU.mult).then_inc(xn_ok, 1)

            variances([0])
            normalise(1, 0, TT)
            dve.wait_ge(id_ok, 1)
            link(dve.tensor_reduce(stack[:, :], ident[:, :].rearrange("p (g c) -> p c g", g=NG), AX_X, ALU.add))
            dve.sem_inc(stack_ok, 1)
            dve.wait_ge(a_exp, 1)
            dve.tensor_scalar(a_neg[:, :], a_neg[:, :], -1.0, None, ALU.mult).then_inc(a_ok, 1)

            variances(list(range(1, NCH)))
            normalise(2, TT, NCH * TT)
            per_chunk = "p (c j) e -> p c j e"

            def route_ranks(lo, hi):
                if lo == 0:
                    dve.wait_ge(lg_mm, 1)
                    link(dve.tensor_copy(logit[:, :, :].rearrange(per_chunk, j=TT),
                                         dt_ps[:, :].rearrange("p (j c f) -> p c j f", c=NCH, f=CH)[:, :, :, 0:E]))
                    link(dve.tensor_reduce(m1, logit[:, :, :], AX_X, ALU.max))
                    link(dve.memset(rank[:, :, :], 0.0))
                for e in range(lo, hi):
                    if e:
                        dve.tensor_tensor(cmp_[:, :, 0:e], logit[:, :, e:e + 1].broadcast_to([P, 16, e]),
                                          logit[:, :, 0:e], ALU.is_gt).then_inc(dve_link, 1)
                        links[0] += 1
                    dve.tensor_tensor(cmp_[:, :, e:E], logit[:, :, e:e + 1].broadcast_to([P, 16, E - e]),
                                      logit[:, :, e:E], ALU.is_ge).then_inc(dve_link, 1)
                    links[0] += 1
                    dve.wait_ge(dve_link, links[0])
                    link(dve.tensor_tensor(rank[:, :, :], rank[:, :, :], cmp_[:, :, :], ALU.add))
                if hi < E:
                    return
                link(dve.tensor_tensor(logit[:, :, :], logit[:, :, :],
                                       m1.rearrange("p (t o) -> p t o", o=1).broadcast_to([P, 16, E]),
                                       ALU.subtract))
                dve.sem_inc(lg_d, 1)
                link(dve.tensor_scalar(first[:, :, :], rank[:, :, :], 1.0, None, ALU.is_le))
                link(dve.tensor_scalar(both[:, :, :], rank[:, :, :], 2.0, None, ALU.is_le))
                dve.sem_inc(pick_ok, 1)

            def route_rows():
                dve.wait_ge(pos_mm, 1)
                earlier = y_ps[:, 0, 0:128].rearrange("p (t e) -> p t e", e=E)
                in_tile = y_ps[:, 0, 128:256].rearrange("p (c j e) -> p c j e", j=TT, e=E)
                ah = ahead[:, :, :].rearrange(per_chunk, j=TT)
                link(dve.memset(ahead[:, :, :], 0.0))
                for j in range(1, TT):
                    link(dve.tensor_tensor(ah[:, :, j, :], ah[:, :, j - 1, :], in_tile[:, :, j - 1, :], ALU.add))
                link(dve.tensor_tensor(count[:, :, :], ah[:, :, TT - 1, :], in_tile[:, :, TT - 1, :], ALU.add))
                link(dve.tensor_scalar(tiles[:, :, :], count[:, :, :], 0.0, None, ALU.is_gt))
                for j in range(1, TT):
                    link(dve.scalar_tensor_tensor(out=tiles[:, :, :], in0=count[:, :, :], scalar=float(P * j),
                                                  in1=tiles[:, :, :], op0=ALU.is_gt, op1=ALU.add))
                link(dve.memset(tile0[:, :, :], 0.0))
                for e in range(1, E):
                    link(dve.tensor_tensor(tile0[:, :, e], tile0[:, :, e - 1], tiles[:, :, e - 1], ALU.add))
                link(dve.tensor_tensor(tile1[:, :, :], tile0[:, :, :], tiles[:, :, :], ALU.add))
                link(dve.tensor_tensor(pos[:, :, :], ahead[:, :, :], earlier, ALU.add))
                for c in range(NCH):
                    link(dve.scalar_tensor_tensor(out=pos[:, TT * c:TT * (c + 1), :],
                                                  in0=tile0[:, c:c + 1, :].broadcast_to([P, TT, E]), scalar=float(P),
                                                  in1=pos[:, TT * c:TT * (c + 1), :], op0=ALU.mult, op1=ALU.add))
                link(dve.tensor_tensor(both[:, :, :], both[:, :, :], first[:, :, :], ALU.subtract))
                for pick, r, row in ((first, r1, row1), (both, r2, row2)):
                    link(dve.tensor_tensor(sel[:, :, :], pick[:, :, :], pos[:, :, :], ALU.mult))
                    link(dve.tensor_reduce(r, sel[:, :, :], AX_X, ALU.add))
                    link(dve.tensor_copy(row[:, :], r))
                for c in range(NCH):
                    link(dve.tensor_tensor(past[:, c, :, :], tile1[:, c:c + 1, :].broadcast_to([P, SLOTS, E]),
                                           slot_no.rearrange("p (j o) -> p j o", o=1).broadcast_to([P, SLOTS, E]),
                                           ALU.is_le))
                link(dve.tensor_reduce(e_no, past.rearrange("p c j e -> p (c j) e"), AX_X, ALU.add))
                link(dve.tensor_scalar(e_no, e_no, float(E - 1), float(P), ALU.min, ALU.mult))
                link(dve.tensor_copy(e_row[:, :], e_no))
                dve.sem_inc(slot_ok, 1)

            def route_weights():
                dve.wait_ge(lg_e, 1)
                for pick, e_sum in ((first, e1), (both, e2)):
                    link(dve.tensor_tensor(sel[:, :, :], pick[:, :, :], logit[:, :, :], ALU.mult))
                    link(dve.tensor_reduce(e_sum, sel[:, :, :], AX_X, ALU.add))
                link(dve.tensor_tensor(r1, e1, e2, ALU.add))
                link(dve.reciprocal(r1, r1))
                link(dve.tensor_tensor(p1[:, :], e1, r1, ALU.mult))
                dve.tensor_tensor(p2[:, :], e2, r1, ALU.mult).then_inc(prob_ok, 1)

            def convolve(c, t, at):
                j = NT * c + t
                dve.wait_ge(tap_ok, j + 1)
                for k in range(1, K):
                    if k > 1:
                        dve.wait_ge(dve_link, at + k - 1)
                    if k == K - 1:
                        dve.wait_ge(halo_ok, j + 1)
                    last = dve.scalar_tensor_tensor(out=z[:, :], in0=x_pad[:, k:k + TC],
                                                    scalar=cw[:, bass.ds(t * K + k, 1)], in1=z[:, :],
                                                    op0=ALU.mult, op1=ALU.add)
                    last.then_inc(dve_link if k < K - 1 else conv_ok, 1)
            CONV_LINKS = K - 2

            def first_convolutions(lo, hi):
                base = links[0] - CONV_LINKS * lo
                with dve.Fori(lo, hi) as t:
                    convolve(0, t, base + CONV_LINKS * t)
                links[0] += CONV_LINKS * (hi - lo)

            dve.wait_ge(dve_link, links[0])
            first_convolutions(0, 3)
            route_ranks(0, E // 2)
            first_convolutions(3, 4)
            route_ranks(E // 2, E)
            first_convolutions(4, NT)
            route_rows()

            def step_sizes(c, t, at):
                n = NT * c + t
                dve.wait_ge(dt_ln, 2 * (n + 1))
                dve.scalar_tensor_tensor(out=dt[:, :], in0=dt[:, :], scalar=-1.0, in1=t_e[:, :],
                                         op0=ALU.add, op1=ALU.subtract).then_inc(dve_link, 1)
                dve.wait_ge(dve_link, at + 1)
                dve.tensor_tensor(t_l[:, :], t_l[:, :], dt[:, :], ALU.subtract).then_inc(dve_link, 1)
                dve.wait_ge(dve_link, at + 2)
                dve.scalar_tensor_tensor(out=dt[:, :], in0=dt_ps[:, :], scalar=0.0, in1=t_l[:, :],
                                         op0=ALU.max, op1=ALU.add).then_inc(dve_link, 1)
                dve.wait_ge(dve_link, at + 3)
                dve.wait_ge(x_ok, START + NT * c + t + 1)
                dve.tensor_tensor(u[:, :], dt[:, :], xy[:, c % 2, t, :], ALU.mult).then_inc(dt_ok, 1)
            DT_LINKS = 3

            def step_sizes_and_convolve(c, t, at):
                n = NT * c + t + 1
                j = NT * (c + 1) + t

                def tap(k):
                    return dve.scalar_tensor_tensor(out=z[:, :], in0=x_pad[:, k:k + TC],
                                                    scalar=cw[:, bass.ds(t * K + k, 1)], in1=z[:, :],
                                                    op0=ALU.mult, op1=ALU.add)
                dve.wait_ge(dt_ln, 2 * (n + 1))
                dve.scalar_tensor_tensor(out=dt[:, :], in0=dt[:, :], scalar=-1.0, in1=t_e[:, :],
                                         op0=ALU.add, op1=ALU.subtract).then_inc(dve_link, 1)
                dve.wait_ge(tap_ok, j + 1)
                tap(1).then_inc(dve_link, 1)
                dve.wait_ge(dve_link, at + 1)
                dve.tensor_tensor(t_l[:, :], t_l[:, :], dt[:, :], ALU.subtract).then_inc(dve_link, 1)
                dve.wait_ge(dve_link, at + 2)
                tap(2).then_inc(dve_link, 1)
                dve.wait_ge(dve_link, at + 3)
                dve.scalar_tensor_tensor(out=dt[:, :], in0=dt_ps[:, :], scalar=0.0, in1=t_l[:, :],
                                         op0=ALU.max, op1=ALU.add).then_inc(dve_link, 1)
                dve.wait_ge(dve_link, at + 4)
                dve.wait_ge(halo_ok, j + 1)
                tap(3).then_inc(conv_ok, 1)
                dve.wait_ge(dve_link, at + 5)
                dve.wait_ge(x_ok, START + n + 1)
                dve.tensor_tensor(u[:, :], dt[:, :], xy[:, c % 2, t + 1, :], ALU.mult).then_inc(dt_ok, 1)

            def quad(c, t, r):
                n = NT * c + t
                m = NR * n + r
                d0, u0 = NQ * r, NQ * (r % DRIVES)
                for q in range(NQ):
                    dve.wait_ge(decay_ok, UNITS * n + NQ * r + q + 1)
                    dve.wait_ge(drive_ok, UNITS * n + NQ * r + q + 1)
                    dve.tensor_tensor_scan(drive[:, u0 + q, :], decay[:, d0 + q, :], drive[:, u0 + q, :],
                                           state[:, bass.ds(t * UNITS + r * NQ + q, 1)],
                                           ALU.mult, ALU.add).then_inc(scan_ok, 1)
                dve.wait_ge(scan_ok, NQ * (m + 1))
                dve.tensor_scalar(state[:, bass.ds(t * UNITS + r * NQ, NQ)], drive[:, u0:u0 + NQ, TC - 1], 1.0, None,
                                  ALU.mult).then_inc(dve_link, 1)
                if is_zero(t) and r == 0:
                    dve.wait_ge(s_c, 16 * NG * (c + 1))
                dve.tensor_tensor(decay[:, d0:d0 + NQ, :], drive[:, u0:u0 + NQ, :], c_all[:, :, :],
                                  ALU.mult).then_inc(prod_ok, 1)

            def gate_tile(c, t, s):
                n = NT * c + t
                dve.wait_ge(sum_ok, DECAYS + NR * (n + 1))
                dve.wait_ge(g_ok, START + n + 1)
                dve.tensor_tensor(xy[:, c % 2, t, :], y_ps[:, s, :], gate[:, :], ALU.mult).then_inc(gated, 1)

            def combine(c):
                for i in range(TT):
                    k = TT * c + i
                    dve.wait_ge(scaled, k + 1)
                    dve.scalar_tensor_tensor(out=moe[:, i, :], in0=second[i], scalar=p2[:, k:k + 1], in1=moe[:, i, :],
                                             op0=ALU.mult, op1=ALU.add).then_inc(comb_ok, 1)

            def out_tile(c, i):
                k = TT * c + i
                dve.wait_ge(o_mm, k + 1)
                dve.wait_ge(moe_ok, k + 1)
                dve.tensor_tensor(moe[:, i, :], out_bank(c, i), moe[:, i, :], ALU.mult).then_inc(o_mul, 1)

            def mid(c):
                dve.wait_ge(ssm_r, c + 1)
                r, tmp = t_l[0:SSM, :], y_t[0:SSM, :]
                link(dve.scalar_tensor_tensor(out=tmp, in0=dt_ps[0:SSM, :], scalar=RMS_EPS, in1=r,
                                              op0=ALU.add, op1=ALU.mult))
                link(dve.tensor_tensor(tmp, tmp, r, ALU.mult))
                link(dve.scalar_tensor_tensor(out=tmp, in0=tmp, scalar=-3.0, in1=r, op0=ALU.add, op1=ALU.mult))
                if c:
                    dve.wait_ge(s_bc0, 16 * c)
                    dve.wait_ge(dt_mm, NT * c)
                dve.scalar_tensor_tensor(out=dt_in[0:SSM, :], in0=tmp, scalar=-0.5, in1=o_ps[0:SSM, :],
                                         op0=ALU.mult, op1=ALU.mult).then_inc(dtin_ok, 1)

            def first_step_sizes(c):
                step_sizes(c, 0, links[0])
                links[0] += DT_LINKS

            mid(0)
            first_step_sizes(0)
            for c in range(NCH):
                dve.wait_ge(s_b, 16 * NG * (c + 1))
                dve.wait_ge(s_rep[0], REP * (NT * c + 1))
                if c:
                    dve.wait_ge(prod_ok, DRIVES + NR * NT * c)
                dve.tensor_tensor(drive[:, 0:NQ, :], rep[:, 0, 1:2, :].broadcast_to([P, NQ, TC]), b_all[:, :, :],
                                  ALU.mult).then_inc(drive0_ok, 1)
                dve.wait_ge(drive0_ok, c + 1)
                conv = CONV_LINKS if c < NCH - 1 else 0
                per_pair = 2 * (NR + DT_LINKS + conv)

                def body(pr, first, last, c=c, conv=conv, per_pair=per_pair):
                    at = links[0] if first or last else links[0] + (pr - 1) * per_pair
                    for s in range(2):
                        t = pr * 2 + s
                        quad(c, t, 0)
                        at = at + 1
                        if first and s == 1 and c:
                            out_tile(c - 1, 2)
                        end = last and s == 1
                        if conv and end:
                            gate_tile(c, t - 1, 1 - s)
                            convolve(c + 1, t, at)
                            at = at + conv
                        quad(c, t, 1)
                        at = at + 1
                        if not (first and s == 0) and not (conv and end):
                            gate_tile(c, t - 1, 1 - s)
                        if first and s == 1 and c:
                            out_tile(c - 1, 3)
                        if conv and first and s == 1 and c:
                            step_sizes(c, t + 1, at)
                            at = at + DT_LINKS
                            convolve(c + 1, t, at)
                            at = at + conv
                        elif conv and not end:
                            step_sizes_and_convolve(c, t, at)
                            at = at + DT_LINKS + conv
                        elif not end:
                            step_sizes(c, t + 1, at)
                            at = at + DT_LINKS
                        if end and conv:
                            links[0] = at
                            if (c + 1) % PER_ROW == PER_ROW - 1:
                                link(dve.memset(halo[:, :, :], 0.0))
                            mid(c + 1)
                            at = links[0]
                        quad(c, t, 2)
                        at = at + 1
                        if first and s == 0 and c:
                            combine(c - 1)
                        if end and conv:
                            links[0] = at
                            first_step_sizes(c + 1)
                            at = links[0]
                        quad(c, t, 3)
                        at = at + 1
                        if first and s == 0:
                            if c:
                                out_tile(c - 1, 0)
                                out_tile(c - 1, 1)
                            else:
                                links[0] = at
                                route_weights()
                                at = links[0]
                    if last and (c + 1) % PER_ROW == 0 and conv:
                        links[0] = at
                        dve.wait_ge(dve_link, at)
                        link(dve.memset(state[:, :], 0.0))
                        at = links[0]
                    if last:
                        gate_tile(c, t, 1)
                    if first:
                        links[0] = at
                    elif last:
                        links[0] = at
                    else:
                        links[0] = links[0] + per_pair * (PAIRS - 2)
                in_pairs(dve, body)
            combine(NCH - 1)
            for i in range(TT):
                out_tile(NCH - 1, i)

        @block.tensor
        def _(pe):
            pe.sem_inc(sum_ok, DECAYS)
            pe.wait_ge(id_ok, 1)

            def transposes(tiles):
                for k in tiles:
                    pe.wait_ge(xn_ok, k + 1)
                    if k >= 2:
                        pe.wait_ge(tr_ev, k - 1)
                    for h in range(HK):
                        last = pe.transpose(f_ps[:, k % 2, P * h:P * (h + 1)], decay[:, k, P * h:P * (h + 1)],
                                            ident[:, :])
                    last.then_inc(tr_mm, 1)

            def router_logits():
                for h in range(HK):
                    for c in range(NCH):
                        last = pe.matmul(g_ps[CH * c:CH * (c + 1), :], w_gate[:, h, :],
                                         xnT[:, h, TC * c:TC * (c + 1)], start=(h == 0), stop=(h == HK - 1))
                last.then_inc(lgT_mm, 1)

            def turn_logits():
                pe.wait_ge(lgT_ok, 1)
                for j in range(TT):
                    last = pe.transpose(dt_ps[:, P * j:P * (j + 1)], logit_T[:, P * j:P * (j + 1)], ident[:, :])
                last.then_inc(lg_mm, 1)

            def count_pairs():
                pe.wait_ge(pick_ok, 1)
                for k, m in enumerate((before, ones)):
                    last = pe.matmul(y_ps[:, 0, P * k:P * (k + 1)], m, both[:, :, :].rearrange("p t e -> p (t e)"),
                                     start=True, stop=True)
                last.then_inc(pos_mm, 1)

            def project_x(c, t, w):
                j = NT * c + t
                pe.wait_ge(x_ev, START + j)
                for h in range(HK):
                    last = pe.matmul(x_ps[:, :], w(h), xnT[:, h, TC * c:TC * (c + 1)],
                                     start=(h == 0), stop=(h == HK - 1))
                last.then_inc(x_mm, 1)

            def add_ssm(c, t, w, first, last):
                pe.wait_ge(x_ok, START + NT * c + t + 1)
                mm = pe.matmul(o_ps[0:SSM, :], w, xy[:, c % 2, t, :], start=first, stop=last)
                if last:
                    mm.then_inc(ssm_mm, 1)

            transposes(range(TT))
            pe.wait_ge(s_const, 16 * 11)
            pe.wait_ge(s_xw, 16)
            pe.wait_ge(tr_ev, TT)
            for t in range(NT):
                project_x(0, t, lambda h: x_w[:, t, P * h:P * (h + 1)])
                if t == 1:
                    transposes(range(TT, NCH * TT))
                    pe.wait_ge(tr_ev, NCH * TT)
                if t:
                    add_ssm(0, t - 1, w_x[:, t - 1, :], t == 1, False)
                if t == 0:
                    continue
                if t == 1:
                    router_logits()
                elif t == 2:
                    turn_logits()
            count_pairs()

            def step_sizes(n, w):
                if not is_zero(n):
                    pe.wait_ge(dt_ok, n)
                pe.matmul(dt_ps[:, :], w, dt_in[:, :], start=True, stop=True).then_inc(dt_mm, 1)

            def out_tile(c, i, lo=0, hi=NT):
                k = TT * c + i
                if i == 0 or lo == 0:
                    pe.wait_ge(gated, START + NT * c + hi)
                if c == NCH - 1:
                    if lo == 0 and i == 0:
                        pe.wait_ge(o_mul, k)
                    elif lo == 0 and i == 2:
                        pe.wait_ge(dt_ok, NT * NCH)
                    elif lo == 0 and i == 3:
                        pe.wait_ge(xt_ev, SLOTS * NCH)
                elif i == 0:
                    if c:
                        pe.wait_ge(o_mul, k)
                    pe.wait_ge(s_wr[1], 16 * 8 * (c + 1))
                elif i == 1:
                    pe.wait_ge(xt_ev, SLOTS * (c + 1))
                    pe.wait_ge(f_ev, SLOTS * (c + 1))
                elif i == 3:
                    pe.wait_ge(o_mul, k - 2)
                for t in range(lo, hi):
                    if c < NCH - 1 and i == 0 and t == HK:
                        pe.wait_ge(s_wr[0], 16 * 9 * (c + 1))
                    if c == NCH - 1 and i == 0 and t % HK == 0:
                        pe.wait_ge(s_wo[t // HK], 16)
                    w = xy[:, 1 - c % 2, t, :] if c == NCH - 1 else w_ring[:, 1 - t // HK, t % HK, :]
                    last = pe.matmul(out_bank(c, i), xy[:, c % 2, t, P * i:P * (i + 1)], w,
                                     start=(t == 0), stop=(t == NT - 1))
                if hi == NT:
                    last.then_inc(o_mm, 1)

            def turn_slot(c, j):
                m = SLOTS * c + j
                pe.wait_ge(s_gx, 16 * (m + 1))
                if not (c == 0 and is_zero(j)):
                    pe.wait_ge(xt_ev, m)
                for h in range(HK):
                    last = pe.transpose(f_ps[:, 0, P * h:P * (h + 1)], x_slot[:, P * h:P * (h + 1)], ident[:, :])
                last.then_inc(xt_mm, 1)

            def expert(c, j, slot, loads):
                m = SLOTS * c + j
                pe.wait_ge(s_wr[slot], 16 * loads)
                pe.wait_ge(xt_ev, m + 1)
                if not (c == 0 and is_zero(j)):
                    pe.wait_ge(f_ev, m)
                for h in range(HK):
                    last = pe.matmul(f_ps[:, 1, :], xT_slot[:, h, :], w_ring[:, slot, h, :],
                                     start=(h == 0), stop=(h == HK - 1))
                last.then_inc(f_mm, 1)

            def skip(c, t, s):
                n = NT * c + t
                pe.wait_ge(diag_ok, n + 1)
                if not is_zero(n):
                    pe.wait_ge(gated, START + n - 1)
                pe.matmul(y_ps[:, s, :], diag[:, :], xy[:, c % 2, t, :], start=True, stop=False).then_inc(skip_mm, 1)

            def sum_states(c, t, s, r):
                m = NR * (NT * c + t) + r
                pe.wait_ge(prod_ok, DRIVES + m + 1)
                for q in range(NQ):
                    last = pe.matmul(y_ps[CH * r:CH * (r + 1), s, :], stack[:, :], decay[:, NQ * r + q, :],
                                     start=False, stop=(q == NQ - 1))
                last.then_inc(sum_ok, 1)

            def mid_means(c):
                add_ssm(c, NT - 1, w_x_last[:, :], False, True)
                if c:
                    pe.wait_ge(dt_ok, NT * c)
                pe.wait_ge(sq_ok, c + 1)
                pe.matmul(dt_ps[0:SSM, :], mean_w[0:SSM, :], t_e[0:SSM, :], start=True, stop=True).then_inc(mean_mm, 1)

            def mid_step_sizes(c):
                pe.wait_ge(dtin_ok, c + 1)
                step_sizes(NT * c, w_dt0[:, :])

            mid_means(0)
            mid_step_sizes(0)
            def next_inputs(c, t, n, last):
                pe.wait_ge(s_rec, 16 * (n + 1))
                if not last:
                    step_sizes(n + 1, w_rec[:, 2 * HK, :])
                if c < NCH - 1:
                    project_x(c + 1, t, lambda h: w_rec[:, h, :])

            def last_chunk(c, t, s):
                a, b = slots_of(c, t)
                loads = [9 * c + t, 8 * c + t] if t == 1 else [8 * c + t, 9 * c + t + 1]
                expert(c, a, a % 2, loads[0])
                turn_slot(c, b)
                sum_states(c, t, s, 0)
                expert(c, b, b % 2, loads[1])
                sum_states(c, t, s, 1)
                if t == 1:
                    turn_slot(c, 2)
                    sum_states(c, t, s, 2)
                    expert(c, 2, 0, 9 * c + 2)
                elif t >= 3:
                    begun = range(t - 3, t - 2 if t < NT - 1 else NT - 1)
                    for i in range(2):
                        out_tile(c, i, begun[0], begun[-1] + 1)
                if t > 1:
                    sum_states(c, t, s, 2)
                if t == NT - 1:
                    out_tile(c, 2, 0, NT - 1)
                sum_states(c, t, s, 3)

            pe.wait_ge(stack_ok, 1)
            for c in range(NCH):
                def body(pr, first, last, c=c):
                    for s in range(2):
                        t = pr * 2 + s
                        n = NT * c + t
                        if not (first and s == 1):
                            next_inputs(c, t, n, last and s == 1)
                        if not (first and s == 0):
                            if first and c:
                                pe.wait_ge(o_mul, TT * (c - 1) + 3)
                            turn_slot(c, slots_of(c, t)[0])
                        if c < NCH - 1:
                            if not (first and s == 0):
                                if first and c:
                                    pe.wait_ge(o_mul, TT * c)
                                add_ssm(c + 1, t - 1, w_rec[:, 2 * HK + 1, 0:SSM], first, False)
                        pe.wait_ge(g_ok, START + n)
                        for h in range(HK):
                            mm = pe.matmul(g_ps[:, :], w_rec[:, HK + h, :], xnT[:, h, TC * c:TC * (c + 1)],
                                           start=(h == 0), stop=(h == HK - 1))
                        mm.then_inc(g_mm, 1)
                        skip(c, t, s)
                        if first and s == 0:
                            for r in range(NR):
                                if r == 2:
                                    next_inputs(c, t + 1, n + 1, False)
                                sum_states(c, t, s, r)
                                if c:
                                    out_tile(c - 1, r)
                            continue
                        if c == NCH - 1:
                            last_chunk(c, t, s)
                            continue
                        end = last and s == 1
                        expert(c, 2 * t - 2, 0, 9 * c + t)
                        if end:
                            mid_means(c + 1)
                        sum_states(c, t, s, 0)
                        turn_slot(c, 2 * t - 1)
                        sum_states(c, t, s, 1)
                        if end:
                            mid_step_sizes(c + 1)
                        expert(c, 2 * t - 1, 1, 8 * c + t)
                        sum_states(c, t, s, 2)
                        if end:
                            turn_slot(c, SLOTS - 1)
                            expert(c, SLOTS - 1, 0, 9 * c + NT)
                        sum_states(c, t, s, 3)
                if c < NCH - 1:
                    in_pairs(pe, body)
                else:
                    for pr in range(PAIRS):
                        body(pr, pr == 0, pr == PAIRS - 1)
            out_tile(NCH - 1, 3, 0, NT - 1)
            for i in range(TT):
                out_tile(NCH - 1, i, NT - 1, NT)


def kernel(**inputs):
    import numpy as np
    import concourse.bacc as bacc
    from concourse.bass_utils import run_bass_kernel_spmd

    v = {k.split("_", 2)[2] if k.startswith("L0") else k: np.asarray(a) for k, a in inputs.items()}
    f = np.float32

    w_in = v["W_in"].reshape(2, NT, P, HK, P).transpose(1, 4, 0, 3, 2).reshape(NT, P, 2 * HK, P)
    w_dt = np.zeros((NT, P, P), f)
    w_dt[:, :R] = v["W_dt"].reshape(NT, P, R).transpose(0, 2, 1)
    w_dt[:, ONES_ROW] = v["b_dt"].reshape(NT, P)
    w_x = v["W_x"].reshape(SSM, NT, P).transpose(1, 2, 0)
    w_x_rec = np.zeros((NT, P, P), f)
    w_x_rec[:, :, :SSM] = w_x
    rec = np.concatenate([w_in, np.roll(w_dt, -1, axis=0)[:, :, None],
                          np.roll(w_x_rec, 1, axis=0)[:, :, None]], axis=2)
    rec = np.concatenate([rec, rec[:1]])
    experts = v["expert_w"].reshape(E, HK, P, H).transpose(0, 2, 1, 3)
    mean_w = np.zeros((SSM, SSM), f)
    for lo, count in ((0, R), (R, N), (R + N, N)):
        mean_w[lo:lo + count, lo:lo + count] = 1.0 / count
    gate_w = np.zeros((H, CH), f)
    gate_w[:, :E] = v["gate_w"]
    consts = np.zeros((P, 2 * P + SLOTS), f)
    consts[:, :P] = np.triu(np.ones((P, P)), 1)
    consts[:, P:2 * P] = 1.0
    consts[:, 2 * P:] = np.arange(SLOTS)
    w_out = v["W_out"].T.reshape(2, HK, P, H).transpose(0, 2, 1, 3)
    arrays = {
        "x": v["hidden_states"].reshape(TOK, H),
        "win": rec,
        "wdt0": w_dt[0],
        "wx": w_x.transpose(1, 0, 2),
        "wring": np.concatenate([experts, w_out]),
        "gate_w": gate_w.reshape(HK, P, CH).transpose(1, 0, 2),
        "means": mean_w,
        "a_log": v["A_log"].reshape(NT * NR, CH, NG, NQ).transpose(2, 1, 0, 3).reshape(P, NT * UNITS),
        "conv_w": v["conv_w"].reshape(NT, P, K).transpose(1, 0, 2).reshape(P, NT * K),
        "conv_b": v["conv_b"].reshape(NT, P).T,
        "d_skip": v["D"].reshape(NT, P).T,
        "w_x7": w_x[NT - 1],
        "token_ids": np.arange(TOK, dtype=np.int32).reshape(TOK // P, P).T,
        "route_consts": consts,
    }
    arrays = {k: np.ascontiguousarray(a) for k, a in arrays.items()}
    nc = bacc.Bacc("TRN2", target_bir_lowering=False, num_devices=1)
    aps = [nc.dram_tensor(k, a.shape, I32 if a.dtype == np.int32 else F32, kind="ExternalInput").ap()
           for k, a in arrays.items()]
    bc = nc.dram_tensor("bc_rows", (NCH, 2 * N, TC), F32, kind="Internal").ap()
    xn_rows = nc.dram_tensor("xn_rows", (TOK, H), F32, kind="Internal").ap()
    order = [nc.dram_tensor(f"order{c}", (ROWS, 1), I32, kind="Internal").ap() for c in range(NCH)]
    slot_rows = [nc.dram_tensor(f"slot_rows{c}", (ROWS, H), F32, kind="Internal").ap() for c in range(NCH)]
    out = nc.dram_tensor("out", (TOK, H), F32, kind="ExternalOutput").ap()
    scan_moe(nc, *aps, bc, xn_rows, order, slot_rows, out)
    r = run_bass_kernel_spmd(nc, [arrays], core_ids=[0])
    return r.results[0]["out"].reshape(BATCH, SEQ, H)
```
